# Optimizing a Trainium2 kernel written in Bass

```python
import numpy as np
import jax
import jax.numpy as jnp

def _softmax(x, axis=-1):
    return jax.nn.softmax(x, axis=axis)

def _gelu(x):
    return jax.nn.gelu(x, approximate=True)

def _silu(x):
    return jax.nn.silu(x)

def _sigmoid(x):
    return jax.nn.sigmoid(x)

def _layernorm(x, axis=-1, eps=1e-05):
    m = jnp.mean(x, axis=axis, keepdims=True)
    v = jnp.var(x, axis=axis, keepdims=True)
    return (x - m) / jnp.sqrt(v + eps)

def _scatter_add(tgt, idx, src, axis=0):
    return tgt.at[idx].add(src)

def _segment_sum(src, seg, n):
    return jax.ops.segment_sum(src, seg, n)
kernel_name = 'mk_adaln_d1_jaxref_r8_21a407'

def setup_inputs(seed: int=0):
    np.random.seed(seed)
    _w = jnp.asarray

    def _L0_attn_setup():
        import jax, jax.numpy as jnp
        import numpy as np
        EPS_FEAT = 1.0 + 0.0001
        EPS_DEN = 1e-06

        def _linear_attention(x, W_qkv, b_qkv, W_out, b_out, num_heads=16):
            B, L, D = x.shape
            H = num_heads
            E = D // H
            qkv = x @ W_qkv + b_qkv
            q, k, v = jnp.split(qkv, 3, axis=-1)
            q = q.reshape(B, L, H, E)
            k = k.reshape(B, L, H, E)
            v = v.reshape(B, L, H, E)
            q = jax.nn.elu(q * E ** (-0.5)) + EPS_FEAT
            k = jax.nn.elu(k) + EPS_FEAT
            qL = jnp.moveaxis(q, 1, 0)
            kL = jnp.moveaxis(k, 1, 0)
            vL = jnp.moveaxis(v, 1, 0)
            kv0 = jnp.zeros((B, H, E, E), dtype=x.dtype)
            ks0 = jnp.zeros((B, H, E), dtype=x.dtype)

            def step(carry, qkv_t):
                kv_s, k_s = carry
                q_t, k_t, v_t = qkv_t
                kv_s = kv_s + jnp.einsum('bhe,bhf->bhef', k_t, v_t)
                k_s = k_s + k_t
                num = jnp.einsum('bhe,bhef->bhf', q_t, kv_s)
                den = jnp.einsum('bhe,bhe->bh', q_t, k_s)[..., None] + EPS_DEN
                return ((kv_s, k_s), num / den)
            _, out = jax.lax.scan(step, (kv0, ks0), (qL, kL, vL))
            out = jnp.moveaxis(out, 0, 1).reshape(B, L, D)
            return out @ W_out + b_out
        key = jax.random.key(seed)
        k1, k2, k3 = jax.random.split(key, 3)
        B, L, D = (4, 512, 128)
        x = jax.random.normal(k1, (B, L, D), dtype=jnp.float32)
        W_qkv = jax.random.normal(k2, (D, 3 * D), dtype=jnp.float32) / np.sqrt(D)
        b_qkv = jnp.zeros((3 * D,), dtype=jnp.float32)
        W_out = jax.random.normal(k3, (D, D), dtype=jnp.float32) / np.sqrt(D)
        b_out = jnp.zeros((D,), dtype=jnp.float32)
        return {'x': x, 'W_qkv': W_qkv, 'b_qkv': b_qkv, 'W_out': W_out, 'b_out': b_out}
    _L0_attn_in = _L0_attn_setup()

    def _L0_ffn_setup():
        import jax, jax.numpy as jnp
        import numpy as np
        B, S, D = (4, 512, 128)
        H = 512
        RH = 128
        E = 16
        K = 2
        NS = 1

        def _swiglu(x, w1, w2, w3):
            return jax.nn.silu(x @ w1) * (x @ w2) @ w3
        key = jax.random.key(seed)
        ks = jax.random.split(key, 9)
        s = 0.02
        return {'x': jax.random.normal(ks[0], (B, S, D), dtype=jnp.float32), 'router_w': jax.random.normal(ks[1], (D, E), dtype=jnp.float32) * s, 'expert_bias': jnp.zeros((E,), dtype=jnp.float32), 'shared_w1': jax.random.normal(ks[2], (NS, D, H), dtype=jnp.float32) * s, 'shared_w2': jax.random.normal(ks[3], (NS, D, H), dtype=jnp.float32) * s, 'shared_w3': jax.random.normal(ks[4], (NS, H, D), dtype=jnp.float32) * s, 'routed_w1': jax.random.normal(ks[5], (E, D, RH), dtype=jnp.float32) * s, 'routed_w2': jax.random.normal(ks[6], (E, D, RH), dtype=jnp.float32) * s, 'routed_w3': jax.random.normal(ks[7], (E, RH, D), dtype=jnp.float32) * s}
    _L0_ffn_in = _L0_ffn_setup()
    _L0_c = _w((lambda *s: np.random.randn(*s).astype(np.float32) * 0.05)(32, 128))
    _L0_wmod = _w((lambda *s: np.random.randn(*s).astype(np.float32) * 0.05)(128, 6 * 128) * 128 ** (-0.5))
    _d = {'L0_attn_x': _L0_attn_in['x'], 'L0_attn_W_qkv': _L0_attn_in['W_qkv'], 'L0_attn_b_qkv': _L0_attn_in['b_qkv'], 'L0_attn_W_out': _L0_attn_in['W_out'], 'L0_attn_b_out': _L0_attn_in['b_out'], 'L0_ffn_router_w': _L0_ffn_in['router_w'], 'L0_ffn_expert_bias': _L0_ffn_in['expert_bias'], 'L0_ffn_shared_w1': _L0_ffn_in['shared_w1'], 'L0_ffn_shared_w2': _L0_ffn_in['shared_w2'], 'L0_ffn_shared_w3': _L0_ffn_in['shared_w3'], 'L0_ffn_routed_w1': _L0_ffn_in['routed_w1'], 'L0_ffn_routed_w2': _L0_ffn_in['routed_w2'], 'L0_ffn_routed_w3': _L0_ffn_in['routed_w3'], 'L0_c': _L0_c, 'L0_wmod': _L0_wmod}
    _x0 = _d['L0_attn_x']
    _d['L0_attn_x'] = jax.random.normal(jax.random.fold_in(jax.random.key(seed), 1), (32, 256, 128), dtype=_x0.dtype)
    del _x0
    return _d

def reference(L0_attn_x, L0_attn_W_qkv, L0_attn_b_qkv, L0_attn_W_out, L0_attn_b_out, L0_ffn_router_w, L0_ffn_expert_bias, L0_ffn_shared_w1, L0_ffn_shared_w2, L0_ffn_shared_w3, L0_ffn_routed_w1, L0_ffn_routed_w2, L0_ffn_routed_w3, L0_c, L0_wmod):

    def _L0_attn_ref(x, W_qkv, b_qkv, W_out, b_out):
        import jax, jax.numpy as jnp
        import numpy as np
        EPS_FEAT = 1.0 + 0.0001
        EPS_DEN = 1e-06

        def _linear_attention(x, W_qkv, b_qkv, W_out, b_out, num_heads=16):
            B, L, D = x.shape
            H = num_heads
            E = D // H
            qkv = x @ W_qkv + b_qkv
            q, k, v = jnp.split(qkv, 3, axis=-1)
            q = q.reshape(B, L, H, E)
            k = k.reshape(B, L, H, E)
            v = v.reshape(B, L, H, E)
            q = jax.nn.elu(q * E ** (-0.5)) + EPS_FEAT
            k = jax.nn.elu(k) + EPS_FEAT
            qL = jnp.moveaxis(q, 1, 0)
            kL = jnp.moveaxis(k, 1, 0)
            vL = jnp.moveaxis(v, 1, 0)
            kv0 = jnp.zeros((B, H, E, E), dtype=x.dtype)
            ks0 = jnp.zeros((B, H, E), dtype=x.dtype)

            def step(carry, qkv_t):
                kv_s, k_s = carry
                q_t, k_t, v_t = qkv_t
                kv_s = kv_s + jnp.einsum('bhe,bhf->bhef', k_t, v_t)
                k_s = k_s + k_t
                num = jnp.einsum('bhe,bhef->bhf', q_t, kv_s)
                den = jnp.einsum('bhe,bhe->bh', q_t, k_s)[..., None] + EPS_DEN
                return ((kv_s, k_s), num / den)
            _, out = jax.lax.scan(step, (kv0, ks0), (qL, kL, vL))
            out = jnp.moveaxis(out, 0, 1).reshape(B, L, D)
            return out @ W_out + b_out
        return _linear_attention(x, W_qkv, b_qkv, W_out, b_out)

    def _L0_ffn_ref(x, router_w, expert_bias, shared_w1, shared_w2, shared_w3, routed_w1, routed_w2, routed_w3):
        import jax, jax.numpy as jnp
        import numpy as np
        B, S, D = (4, 512, 128)
        H = 512
        RH = 128
        E = 16
        K = 2
        NS = 1

        def _swiglu(x, w1, w2, w3):
            return jax.nn.silu(x @ w1) * (x @ w2) @ w3
        shared_out = jnp.sum(jax.vmap(lambda w1, w2, w3: _swiglu(x, w1, w2, w3))(shared_w1, shared_w2, shared_w3), axis=0)
        scores = jax.nn.sigmoid(x @ router_w)
        sel_scores = scores + expert_bias
        _, top_idx = jax.lax.top_k(sel_scores, K)
        top_scores = jnp.take_along_axis(scores, top_idx, axis=-1)
        gates = jnp.sum(jax.nn.one_hot(top_idx, E, dtype=scores.dtype) * top_scores[..., None], axis=-2)
        xf = x.reshape(-1, D)
        gf = gates.reshape(-1, E).T

        def body(acc, ws):
            w1, w2, w3, g = ws
            return (acc + _swiglu(xf, w1, w2, w3) * g[:, None], None)
        routed_out, _ = jax.lax.scan(body, jnp.zeros_like(xf), (routed_w1, routed_w2, routed_w3, gf))
        return shared_out + routed_out.reshape(x.shape)
    x = L0_attn_x
    mod = (_silu(L0_c) @ L0_wmod).reshape(L0_c.shape[0], 6, 1, -1)
    sa, ca, ga, sb, cb, gb = (mod[:, 0], mod[:, 1], mod[:, 2], mod[:, 3], mod[:, 4], mod[:, 5])
    ga = (2 * (ga >= 0) - 1) * jnp.maximum(jnp.abs(ga), 0.25)
    gb = (2 * (gb >= 0) - 1) * jnp.maximum(jnp.abs(gb), 0.25)
    h = _layernorm(x, axis=-1) * (1 + ca) + sa
    x = x + ga * _L0_attn_ref(h, L0_attn_W_qkv, L0_attn_b_qkv, L0_attn_W_out, L0_attn_b_out)
    h = _layernorm(x, axis=-1) * (1 + cb) + sb
    x = x + gb * _L0_ffn_ref(h, L0_ffn_router_w, L0_ffn_expert_bias, L0_ffn_shared_w1, L0_ffn_shared_w2, L0_ffn_shared_w3, L0_ffn_routed_w1, L0_ffn_routed_w2, L0_ffn_routed_w3)
    return x

_drawn_inputs = setup_inputs


def setup_inputs(seed=0):
    import zlib

    import numpy as np

    out = dict(_drawn_inputs(seed))
    spreads = {'L0_attn_b_qkv': (0.0, 0.309),
     'L0_attn_b_out': (0.0, 0.341),
     'L0_ffn_expert_bias': (0.0, 0.8)}
    factors = {'L0_ffn_router_w': 8.0,
     'L0_ffn_shared_w1': 8.0,
     'L0_ffn_shared_w2': 8.0,
     'L0_ffn_shared_w3': 8.0,
     'L0_ffn_routed_w1': 8.0,
     'L0_ffn_routed_w2': 8.0,
     'L0_ffn_routed_w3': 8.0}
    for name, (base, spread) in spreads.items():
        noise = np.random.default_rng([zlib.crc32(name.encode()), seed]).standard_normal(out[name].shape)
        drawn = base * np.exp(spread * noise) if base else spread * noise
        out[name] = jnp.asarray(drawn.astype(out[name].dtype))
    for name, factor in factors.items():
        out[name] = (out[name] * factor).astype(out[name].dtype)
    return out
```

```python
from contextlib import ExitStack

import concourse.bass as bass
from concourse import mybir

F32 = mybir.dt.float32
BF16 = mybir.dt.bfloat16
U32 = mybir.dt.uint32
I32 = mybir.dt.int32
ALU = mybir.AluOpType
ACT = mybir.ActivationFunctionType
AX_X = mybir.AxisListType.X

P = 128
D = 128
NSEQ, L = 32, 256
TPS = L // P
NTILE = NSEQ * TPS
NTOK = NSEQ * L
H, E = 16, 8
NE, RH, TOPK = 16, 128, 2
SH = 512
SM = SH // P
EPS_FEAT, EPS_DEN, EPS_LN = 1e-4, 1e-6, 1e-5
QSCALE = float(E) ** -0.5

BSEQ = 2
BT = BSEQ * TPS
UNROLL = 2 * BSEQ
ROW = D + 4
C_ID, C_E1, C_G1, C_G2 = D, D + 1, D + 2, D + 3
CAP = NTOK + P
SURPLUS = NE * CAP
RT = NTOK * TOPK // P + NE
GT = 4
UNROLL_C = 4
NG = RT // GT
YROWS = NTOK * TOPK + 2 * NE * P
FC = 4


def adaln_block(nc, x, w_qkv, b_qkv, w_out, b_out, router_w, expert_bias,
                sw1, sw2, sw3, rw1, rw2, rw3, c, wmod, out):
    with ExitStack() as ctx:
        def sb(name, shape, dt=F32):
            return ctx.enter_context(nc.sbuf_tensor(name, shape, dt))

        def sem(name):
            return ctx.enter_context(nc.semaphore(name))

        lists = nc.dram_tensor("lists", [SURPLUS + NE * P, ROW], F32, kind="Internal").ap()
        routed = nc.dram_tensor("routed", [YROWS, D], F32, kind="Internal").ap()

        resid = sb("resid", [P, NTILE, D])
        h2T = sb("h2T", [D, NTOK])
        gb_rows = sb("gb_rows", [P, NSEQ, D])
        wqkv_sb = sb("wqkv_sb", [D, 3 * D])
        wout_sb = sb("wout_sb", [P, 2, D])
        wmod_sb = h2T[:, 0:6 * D]
        router_sb = sb("router_sb", [D, NE])
        bias_rows = sb("bias_rows", [P, NE])
        sw1_sb = sb("sw1_sb", [D, SH])
        sw2_sb = sb("sw2_sb", [D, SH])
        sw3_sb = sb("sw3_sb", [P, SM, D])
        rw1_sb = sb("rw1_sb", [D, NE * RH])
        rw2_sb = sb("rw2_sb", [D, NE * RH])
        rw3_sb = sb("rw3_sb", [RH, NE * D])
        ident = sb("ident", [P, P])
        pick_f = sb("pick_f", [P, E, P])
        head_sel = sb("head_sel", [P, 32])
        tri = sb("tri", [P, P], BF16)
        ones_bf = sb("ones_bf", [P, P], BF16)
        ones = sb("ones", [P, L])
        eio = sb("eio", [P, NE])
        expert_base = sb("expert_base", [P, NE])
        tok_id = sb("tok_id", [P, NTILE])
        minus_half = sb("minus_half", [P, TPS])
        fill = sb("fill", [P, NE, ROW])
        c_sb = sb("c_sb", [NSEQ, D])
        c_exp = sb("c_exp", [NSEQ, D])
        c_silu = sb("c_silu", [NSEQ, D])
        cT = sb("cT", [D, NSEQ])
        mod = sb("mod", [D, 6, NSEQ])
        mod_abs = sb("mod_abs", [D, NSEQ])
        mod_sign = sb("mod_sign", [D, NSEQ])
        ga_bout = sb("ga_bout", [D, NSEQ])
        bcol = sb("bcol", [P, 4])
        q_bias = sb("q_bias", [P, 1])
        q_bias1 = sb("q_bias1", [P, 1])
        k_bias1 = sb("k_bias1", [P, 1])
        pool_note = sb("pool_note", [1, 1])
        carrier_dve = sb("carrier_dve", [1, 1])
        carrier_pool = sb("carrier_pool", [1, 1])
        stats = sb("stats", [P, 2, TPS, 6])
        mv1 = sb("mv1", [P, TPS, 2])
        var1 = sb("var1", [P, TPS])
        rstd1 = sb("rstd1", [P, TPS])
        pairs_a = sb("pairs_a", [P, 6, 2, L])
        xn1 = pairs_a[:, 0, :, :].rearrange("p b (a d) -> p b a d", a=TPS)
        xn2 = pairs_a[:, 1, :, :].rearrange("p b (a d) -> p b a d", a=TPS)
        hT = pairs_a[:, 2, :, :]
        singles_a = sb("singles_a", [P, 10, L])
        ex = singles_a[:, 0:2, :]
        feat = singles_a[:, 2:4, :]
        qk = pairs_a[:, 3, :, :]
        lnk = singles_a[:, 4, :]
        rk0 = singles_a[:, 5, :]
        rkt = singles_a[:, 6, :]
        rk = singles_a[:, 7, :]
        ratio = pairs_a[:, 4, :, :]
        vT = pairs_a[:, 5, :, :]
        state = sb("state", [P, 2, E + 1, L])
        z = sb("z", [P, 2, E + 1, L])
        rden = sb("rden", [P, TPS, 32])
        den = sb("den", [P, TPS, H])
        rdenT = sb("rdenT", [P, L])
        num = singles_a[:, 8:10, :]
        attT = sb("attT", [D, L])
        mv2 = sb("mv2", [P, TPS, 2])
        var2 = sb("var2", [P, TPS])
        rstd2 = sb("rstd2", [P, TPS])
        h2 = sb("h2", [D, 2, L])
        rows = sb("rows", [P, 2, BT, ROW])
        rexp = sb("rexp", [P, 2, BT, NE])
        score1 = sb("score1", [P, BT, NE])
        score = sb("score", [P, BT, NE])
        sel = sb("sel", [P, BT, NE])
        top = sb("top", [P, BT, 8])
        topi = sb("topi", [P, BT, 8], U32)
        topf = sb("topf", [P, BT, TOPK])
        onehot = sb("onehot", [P, TOPK, BT, NE])
        chosen = sb("chosen", [P, BT, NE], BF16)
        gtmp = sb("gtmp", [P, TOPK, BT, NE])
        carry = sb("carry", [P, NE])
        place = sb("place", [P, BT, NE])
        ptmp = sb("ptmp", [P, TOPK, BT, NE])
        pos = sb("pos", [P, 2, TOPK, BT], U32)
        cnt = sb("cnt", [P, NE])
        cnt_i = sb("cnt_i", [P, NE], I32)
        nt_f = sb("nt_f", [P, NE])
        nt_i = sb("nt_i", [P, NE], I32)
        nt = sb("nt", [P, NE])
        end = sb("end", [P, NE])
        off = sb("off", [P, NE + 1])
        offt = sb("offt", [P, NE + 1])
        doff = sb("doff", [P, NE])
        jio = sb("jio", [P, RT])
        past = singles_a[:, :, :].rearrange("p a l -> p (a l)")[:, 0:RT * NE].rearrange(
            "p (j e) -> p j e", e=NE)
        et = sb("et", [P, RT])
        etw = sb("etw", [P, RT])
        row0 = sb("row0", [P, RT])
        row0b = sb("row0b", [P, RT])
        et_i = sb("et_i", [P, RT], I32)
        row0_i = sb("row0_i", [P, RT], I32)
        a_state = state[:, :, :, :].rearrange("p a f l -> p (a f l)")
        a_z = z[:, :, :, :].rearrange("p a f l -> p (a f l)")
        W = FC * P
        gate_s = a_state[:, 0:2 * SM * W].rearrange("p (b m t) -> p b m t", b=2, m=SM)
        act_s = a_z[:, 0:2 * W].rearrange("p (b t) -> p b t", b=2)
        xtT = a_z[:, 2 * W:4 * W].rearrange("p (b t) -> p b t", b=2)
        hid = a_z[:, 4 * W:6 * W].rearrange("p (b t) -> p b t", b=2)
        a_pairs = pairs_a[:, :, :, :].rearrange("p a b l -> p (a b l)")
        hidT = a_z[:, 6 * W:8 * W].rearrange("p (b t) -> p b t", b=2)
        xt = a_pairs[:, 0:2 * GT * ROW].rearrange("p (b j r) -> p b j r", b=2, r=ROW)
        yrow = a_pairs[:, 2 * GT * ROW:2 * GT * (ROW + D)].rearrange("p (b j d) -> p b j d", b=2, d=D)
        gb_abs, gb_sign = (a_z[:, k * W:(k + 1) * W].rearrange("p (k d) -> p k d", d=D) for k in range(2))
        sh_mul = sb("sh_mul", [P, FC, D])
        first = sb("first", [P, GT])
        gdiff = sb("gdiff", [P, GT])
        gsel = sb("gsel", [P, GT])
        gate = sb("gate", [P, UNROLL_C, GT])
        dest = sb("dest", [P, UNROLL_C, GT], U32)
        y0, y1, osum = (w[:, 0:2 * W].rearrange("p (b a d) -> p b a d", b=2, d=D)
                        for w in (rw1_sb, rw2_sb, rw3_sb))

        ps = ctx.enter_context(nc.psum_tensor("ps", [P, 8, 512], F32))
        p_hT = ps[:, 0, 0:L]
        p_v = ps[:, 0, L:2 * L]
        p_qk = ps[:, 1, :].rearrange("p (a l) -> p a l", a=2)
        p_rep = ps[:, 2:4, :]
        p_num = ps[:, 4, :].rearrange("p (a l) -> p a l", a=2)
        p_rdT = ps[:, 5, 0:L]
        p_att = ps[:, 5, L:2 * L]
        p_attb = ps[:, 6, 0:L].rearrange("p (a d) -> p a d", a=TPS)
        p_h2T = ps[:, 6, L:2 * L]
        p_back = ps[:, 7, 0:L].rearrange("p (a d) -> p a d", a=TPS)
        p_den = ps[:, 7, L:L + TPS * H].rearrange("p (a h) -> p a h", a=TPS)
        p_log = ps[:, 7, 288:288 + TPS * NE].rearrange("p (a e) -> p a e", a=TPS)
        p_place = ps[:, 7, 320:320 + BT * NE].rearrange("p (a e) -> p a e", a=BT)
        p_total = ps[:, 7, 448:448 + NE]

        names = """w_attn w_mod w_shared w_routed bias_in c_in fill_ok ident_ok pick_ok sel_ok tri_ok
            consts_ok fill_zero fill_cols vconst_ok c_exp_ok c_chain c_silu_ok cT_ps cT_ok mod_ps mod_raw mod_ok
            mod_chain gb_ps gb_ok gb_chain bq_ok wout_zero surplus_out carry0_ok
            stats1 aggr1 veps1 rstd1_ok xn1_ok hT_ps hT_ok qk_ps v_ps exp_ok v_ok exmin_ok feat_ok qk_ok lnk_ok
            rk0_ok rkt_ok rk_ok ratio_ok rep_ps scan_ok z_ok den_ps deneps_ok rden_ok rdT_ps rdT_ok num_ps norm_ok
            att_ps attT_ok attb_ps x1_ok stats2 aggr2 veps2 rstd2_ok xn2_ok h2T_ps h2_ok log_ps
            rowh_ok rexp_ok sc1_ok sc_ok selb_ok top_ok topi_ok topf_ok onehot_ok chosen_ok gtmp_ok rowmeta_ok
            place_ps place_ok ptmp_ok pos_ok carry_ok
            tb cnt_ok tiles_ok fills_out sh_ps sh_act sh_gate sh_out_ps sh_half sh_mul
            xtT_ps xtT_ok hidT_ps hidT_ok hid_ps hid_act hid_ok y_ps y_ok first_ok gdiff_ok gsel_ok gate_ok dest_ok
            osum0 osum1 osum_ok carrier_a carrier_c""".split()
        s = {n: sem(n) for n in names}
        x_in = [sem(f"x_in{i}") for i in range(2)]
        copied = [sem(f"h2_copied{i}") for i in range(2)]
        scat = [sem(f"scattered{i}") for i in range(2)]
        xt_in = [sem(f"xt_in{i}") for i in range(2)]
        yout = [sem(f"y_scattered{i}") for i in range(2)]
        y_in = [sem(f"y_in{i}") for i in range(2)]
        o_out = [sem(f"out_written{i}") for i in range(2)]

        def need(eng, name, n):
            if not isinstance(n, int) or n > 0:
                eng.wait_ge(s[name] if isinstance(name, str) else name, n)

        def need_apart(eng, name, n):
            need(eng, name, n)
            if not isinstance(n, int):
                nc.vector.memset(carrier_dve[:, :], 0.0)

        def need_apart_pool(eng, name, n, written, times):
            need(eng, written, times)
            need(eng, name, n)
            nc.gpsimd.tensor_tensor(carrier_pool[:, :], eio[0:1, 0:1], eio[0:1, 0:1],
                                    ALU.add).then_inc(s[written], 1)

        LA, LB, LC, LD, LE, LR1, LR2 = 0, 1, 2, 3, 4, 5, 6
        LH, LO = 0, 1
        LT, LHID, LG, LY = 0, 1, 2, 3
        LX, LCOPY = 0, 7

        def pipeline(eng, step, count, unroll, lags, head):
            def written_out(t):
                step(t // unroll, t % unroll, lambda lag: 0 <= t - lag < count)
            for t in range(head):
                written_out(t)
            with eng.Fori(head // unroll, count // unroll, 1) as i:
                for u in range(unroll):
                    step(i, u, lambda lag: True)
            for t in range(count, count + lags):
                written_out(t)

        def part_a(eng, step, lags=LR2, head=2 * UNROLL):
            pipeline(eng, step, NSEQ, UNROLL, lags, head)

        def part_b(eng, step):
            pipeline(eng, step, NTILE // FC, 2, LO, 4)

        def part_c(eng, step):
            pipeline(eng, step, NG, UNROLL_C, LY, 2 * UNROLL_C)

        def seq(i, u, lag):
            return i * UNROLL + (u - lag)

        def item(i, u, lag):
            return i * 2 + (u - lag)

        def group(i, u, lag):
            return i * UNROLL_C + (u - lag)

        def turns(i, u, lag, every):
            return i * (UNROLL // every) + (u - lag) // every

        def ends_batch(u, lag):
            return (u - lag) % BSEQ == BSEQ - 1

        def rset(u, lag):
            return ((u - lag) % UNROLL) // BSEQ

        def batches(i, u, lag):
            return turns(i, u, lag, BSEQ) + 1

        def spread(ap, axis, n):
            shape = list(ap.shape)
            return ap.unsqueeze(axis).broadcast_to(shape[:axis] + [n] + shape[axis:])

        block = ctx.enter_context(nc.Block())

        @block.sync
        def _(sp):
            sp.dma_start(c_sb[:, :], c).then_inc(s["c_in"], 16)
            for i in range(2):
                sp.dma_start(resid[:, TPS * i:TPS * i + TPS, :],
                             x[i].rearrange("(a p) d -> p a d", p=P)).then_inc(x_in[i], 16)
            sp.dma_start(wmod_sb[:, :], wmod).then_inc(s["w_mod"], 16)
            sp.dma_start(wqkv_sb[:, :], w_qkv).then_inc(s["w_attn"], 16)
            for i in range(3):
                sp.dma_start(bcol[:, i:i + 1],
                             b_qkv[i * D:(i + 1) * D].rearrange("(p a) -> p a", a=1)).then_inc(s["bias_in"], 16)
            sp.dma_start(bcol[:, 3:4], b_out.rearrange("(p a) -> p a", a=1)).then_inc(s["bias_in"], 16)
            sp.dma_start(bias_rows[:, :], expert_bias.partition_broadcast(P)).then_inc(s["bias_in"], 16)
            sp.wait_ge(s["wout_zero"], 1)
            for f in range(E):
                sp.dma_start(wout_sb[32 * (f % 4):32 * (f % 4) + H, f // 4, :],
                             w_out.rearrange("(h f) d -> f h d", f=E)[f]).then_inc(s["w_attn"], 16)
            sp.dma_start(router_sb[:, :], router_w).then_inc(s["w_attn"], 16)

            sp.wait_ge(s["fill_ok"], 1)
            sp.dma_start(lists[SURPLUS:SURPLUS + NE * P, :].rearrange("(p e) r -> p e r", p=P),
                         fill[:, :, :]).then_inc(s["surplus_out"], 16)

            def step(i, u, on):
                if on(LX) and not (isinstance(i, int) and i == 0 and u < 2):
                    n = turns(i, u, LX, 2)
                    need(sp, x_in[u % 2], n * 16)
                    sp.dma_start(resid[:, bass.ds(seq(i, u, LX) * TPS, TPS), :],
                                 x[bass.ds(seq(i, u, LX), 1)].rearrange("o (a p) d -> p (o a) d", p=P)
                                 ).then_inc(x_in[u % 2], 16)
                if on(LCOPY):
                    q, b = seq(i, u, LCOPY), (u - LCOPY) % 2
                    need(sp, "h2_ok", q + 1)
                    need(sp, copied[b], turns(i, u, LCOPY, 2) * 16)
                    sp.dma_start(h2T[:, bass.ds(q * L, L)], h2[:, b, :]).then_inc(copied[b], 16)

            part_a(sp, step, LCOPY, 3 * UNROLL)
            sp.dma_start(sw1_sb[:, :], sw1[0]).then_inc(s["w_shared"], 16)
            sp.dma_start(sw2_sb[:, :], sw2[0]).then_inc(s["w_shared"], 16)
            sp.dma_start(sw3_sb[:, :, :], sw3[0].rearrange("(m p) d -> p m d", p=P)).then_inc(s["w_shared"], 16)
            sp.dma_start(rw1_sb[:, :].rearrange("p (e r) -> p e r", e=NE),
                         rw1.rearrange("e d r -> d e r")).then_inc(s["w_routed"], 16)
            sp.dma_start(rw2_sb[:, :].rearrange("p (e r) -> p e r", e=NE),
                         rw2.rearrange("e d r -> d e r")).then_inc(s["w_routed"], 16)
            sp.dma_start(rw3_sb[:, :].rearrange("p (e d) -> p e d", e=NE),
                         rw3.rearrange("e r d -> r e d")).then_inc(s["w_routed"], 16)
            sp.wait_ge(s["fill_ok"], 2)
            sp.wait_ge(s["cnt_ok"], 1)
            with sp.Fori(0, NE, 1) as e:
                n = sp.value_load(cnt_i[0:1, bass.ds(e, 1)], min_val=0, max_val=NTOK)
                sp.dma_start(lists[bass.ds(n + e * CAP, P), :].rearrange("(p a) r -> p a r", a=1),
                             fill[:, bass.ds(e, 1), :]).then_inc(s["fills_out"], 16)
            sp.wait_ge(s["fills_out"], 16 * NE)
            sp.wait_ge(s["tiles_ok"], 1)
            for r in range(2):
                sp.wait_ge(scat[r], 16 * TOPK * BT * (NSEQ // BSEQ // 2))

            def load_group(g, par):
                for j in range(GT):
                    r0 = sp.value_load(row0_i[0:1, bass.ds(g * GT + j, 1)], min_val=0,
                                       max_val=SURPLUS + (NE - 1) * P)
                    sp.dma_start(xt[:, par, j:j + 1, :],
                                 lists[bass.ds(r0, P), :].rearrange("(p a) r -> p a r", a=1)
                                 ).then_inc(xt_in[par], 16)

            for par in range(2):
                load_group(par, par)
            with sp.Fori(1, NG // 2, 1) as i:
                for par in range(2):
                    need(sp, "gate_ok", i * 2 + par - 1)
                    need(sp, "dest_ok", i * 2 + par - 1)
                    need(sp, "xtT_ps", i * 2 + par - 1)
                    load_group(i * 2 + par, par)

            for r in range(2):
                sp.wait_ge(yout[r], 16 * GT * (NG // 2))

            def load_y(n, par):
                sp.dma_start(y0[:, par, :, :], routed[bass.ds(n * (FC * P), FC * P), :].rearrange(
                    "(a p) d -> p a d", p=P)).then_inc(y_in[par], 16)
                sp.dma_start(y1[:, par, :, :], routed[bass.ds(n * (FC * P) + NTOK, FC * P), :].rearrange(
                    "(a p) d -> p a d", p=P)).then_inc(y_in[par], 16)

            def store_out(n, par):
                sp.dma_start(out[bass.ds(n * 2, 2)].rearrange("b (a p) d -> p (b a) d", p=P),
                             osum[:, par, :, :]).then_inc(o_out[par], 16)

            load_y(0, 0)
            load_y(1, 1)
            with sp.Fori(0, NTILE // FC // 2 - 1, 1) as i:
                for par in range(2):
                    need(sp, "osum_ok", i * 2 + par + 1)
                    store_out(i * 2 + par, par)
                    load_y(i * 2 + par + 2, par)
            for par in range(2):
                n = NTILE // FC - 2 + par
                need(sp, "osum_ok", n + 1)
                store_out(n, par)
            for par in range(2):
                sp.wait_ge(o_out[par], 16 * (NTILE // FC // 2))

        @block.gpsimd
        def _(gp):
            g = nc.gpsimd
            g.memset(wout_sb[:, :, :], 0.0).then_inc(s["wout_zero"], 1)
            g.memset(ident[:, :], 0.0).then_inc(s["ident_ok"], 1)
            g.memset(pick_f[:, :, :], 0.0).then_inc(s["pick_ok"], 1)
            g.memset(head_sel[:, :], 1.0).then_inc(s["sel_ok"], 1)
            g.memset(tri[:, :], 1.0).then_inc(s["tri_ok"], 1)
            g.memset(ones_bf[:, :], 1.0).then_inc(s["consts_ok"], 1)
            g.memset(ones[:, :], 1.0).then_inc(s["consts_ok"], 1)
            g.memset(minus_half[:, :], -0.5).then_inc(s["consts_ok"], 1)
            g.iota(eio[:, :], [[1, NE]], base=0, channel_multiplier=0,
                   allow_small_or_imprecise_dtypes=True).then_inc(s["consts_ok"], 1)
            g.iota(expert_base[:, :], [[CAP, NE]], base=0, channel_multiplier=0,
                   allow_small_or_imprecise_dtypes=True).then_inc(s["consts_ok"], 1)
            g.iota(tok_id[:, :], [[P, NTILE]], base=NTOK, channel_multiplier=1,
                   allow_small_or_imprecise_dtypes=True).then_inc(s["consts_ok"], 1)
            g.iota(jio[:, :], [[1, RT]], base=0, channel_multiplier=0,
                   allow_small_or_imprecise_dtypes=True).then_inc(s["consts_ok"], 1)
            gp.wait_ge(s["ident_ok"], 1)
            g.affine_select(out=ident[:, :], in_=ident[:, :], compare_op=ALU.not_equal, fill=1.0, base=0,
                            pattern=[[-1, P]], channel_multiplier=1).then_inc(s["ident_ok"], 1)
            gp.wait_ge(s["pick_ok"], 1)
            g.affine_select(out=pick_f[:, :, :].rearrange("p f (h e) -> p f h e", e=E),
                            in_=pick_f[:, :, :].rearrange("p f (h e) -> p f h e", e=E),
                            compare_op=ALU.not_equal, fill=1.0, base=0,
                            pattern=[[-1, E], [-E, H], [0, E]], channel_multiplier=1).then_inc(s["pick_ok"], 1)
            gp.wait_ge(s["sel_ok"], 1)
            g.affine_select(out=head_sel[:, :], in_=head_sel[:, :], compare_op=ALU.is_ge, fill=0.0, base=0,
                            pattern=[[-E, 32]], channel_multiplier=1).then_inc(s["sel_ok"], 1)
            gp.wait_ge(s["sel_ok"], 2)
            g.affine_select(out=head_sel[:, :], in_=head_sel[:, :], compare_op=ALU.is_ge, fill=0.0, base=E - 1,
                            pattern=[[E, 32]], channel_multiplier=-1).then_inc(s["sel_ok"], 1)
            gp.wait_ge(s["tri_ok"], 1)
            g.affine_select(out=tri[:, :], in_=tri[:, :], compare_op=ALU.is_gt, fill=0.0, base=0,
                            pattern=[[1, P]], channel_multiplier=-1).then_inc(s["tri_ok"], 1)
            g.memset(fill[:, :, :], 0.0).then_inc(s["fill_zero"], 1)
            gp.wait_ge(s["fill_zero"], 1)
            g.memset(fill[:, :, C_E1:C_E1 + 1], -1.0).then_inc(s["fill_cols"], 1)
            g.iota(fill[:, :, C_ID:C_ID + 1].rearrange("p e a -> p (e a)"), [[P, NE]], base=NTOK * TOPK + NE * P,
                   channel_multiplier=1, allow_small_or_imprecise_dtypes=True).then_inc(s["fill_cols"], 1)
            gp.wait_ge(s["fill_cols"], 2)
            g.memset(pool_note[:, :], 0.0).then_inc(s["fill_ok"], 1)
            gp.wait_ge(s["surplus_out"], 16)
            g.iota(fill[:, :, C_ID:C_ID + 1].rearrange("p e a -> p (e a)"), [[P, NE]], base=NTOK * TOPK,
                   channel_multiplier=1, allow_small_or_imprecise_dtypes=True).then_inc(s["fill_ok"], 1)

            def step(i, u, on):
                if on(LA):
                    need(gp, "veps1", seq(i, u, LA) + 1)
                    g.tensor_tensor(rstd1[:, :], var1[:, :], minus_half[:, :], ALU.pow).then_inc(s["rstd1_ok"], 1)
                if on(LC):
                    q, b = seq(i, u, LC), (u - LC) % 2
                    need(gp, "qk_ok", q + 1)
                    need(gp, "num_ps", q - 1)
                    need(gp, "den_ps", q - 1)
                    for n, f in enumerate([E] + list(range(E))):
                        need(gp, "scan_ok", q * (E + 1) + n + 1)
                        g.tensor_tensor(z[:, b, f, :], state[:, b, f, :], qk[:, b, :],
                                        ALU.mult).then_inc(s["z_ok"], 1)
                if on(LD):
                    need(gp, "veps2", seq(i, u, LD) + 1)
                    g.tensor_tensor(rstd2[:, :], var2[:, :], minus_half[:, :], ALU.pow).then_inc(s["rstd2_ok"], 1)
                if on(LR2) and ends_batch(u, LR2):
                    r, n = rset(u, LR2), batches(i, u, LR2)
                    need(gp, "rowh_ok", n * BSEQ)
                    need(gp, "rowmeta_ok", n * 3)
                    need_apart_pool(gp, "pos_ok", n, "carrier_a", n - 1)
                    for j in range(BT):
                        for k in range(TOPK):
                            gp.indirect_dma_start(lists, bass.IndirectOffsetOnAxis(pos[:, r, k, j:j + 1], 0),
                                                  rows[:, r, j, :], None).then_inc(scat[r], 16)

            gp.wait_ge(s["consts_ok"], 7)
            part_a(gp, step)

            def put(i, u, on):
                if on(LY):
                    n, par = group(i, u, LY), (u - LY) % 2
                    need(gp, "y_ok", n + 1)
                    need_apart_pool(gp, "dest_ok", n + 1, "carrier_c", n)
                    for j in range(GT):
                        gp.indirect_dma_start(routed, bass.IndirectOffsetOnAxis(dest[:, (u - LY) % UNROLL_C, j:j + 1], 0),
                                              yrow[:, par, j, :], None).then_inc(yout[par], 16)

            gp.wait_ge(s["carrier_a"], NSEQ // BSEQ)
            part_c(gp, put)

        @block.scalar
        def _(act):
            a = nc.scalar
            act.wait_ge(s["c_in"], 16)
            a.activation(c_exp[:, :], c_sb[:, :], ACT.Exp, scale=-1.0).then_inc(s["c_exp_ok"], 1)

            def step(i, u, on):
                if on(LD):
                    q = seq(i, u, LD)
                    need(act, "rdT_ps", q + 1)
                    need(act, "norm_ok", q)
                    a.activation(rdenT[:, :], p_rdT, ACT.Copy).then_inc(s["rdT_ok"], 1)
                if on(LB):
                    q, b = seq(i, u, LB), (u - LB) % 2
                    need(act, "hT_ps", q + 1)
                    need(act, "mod_ok", 1)
                    need(act, "v_ps", q - 1)
                    a.activation(hT[:, b, :], p_hT, ACT.Identity, scale=mod[:, 1, bass.ds(q, 1)],
                                 bias=mod[:, 0, bass.ds(q, 1)]).then_inc(s["hT_ok"], 1)
                if on(LE):
                    q = seq(i, u, LE)
                    b = (u - LE) % 2
                    need(act, "h2T_ps", q + 1)
                    need(act, "log_ps", q - 1)
                    need(act, copied[b], turns(i, u, LE, 2) * 16)
                    a.activation(h2[:, b, :], p_h2T, ACT.Identity, scale=mod[:, 4, bass.ds(q, 1)],
                                 bias=mod[:, 3, bass.ds(q, 1)]).then_inc(s["h2_ok"], 1)
                if on(LD):
                    q = seq(i, u, LD)
                    need(act, "att_ps", q + 1)
                    need(act, "attb_ps", q)
                    a.activation(attT[:, :], p_att, ACT.Identity, scale=mod[:, 2, bass.ds(q, 1)],
                                 bias=ga_bout[:, bass.ds(q, 1)]).then_inc(s["attT_ok"], 1)
                if on(LB):
                    q, b = seq(i, u, LB), (u - LB) % 2
                    need(act, "qk_ps", q + 1)
                    need(act, "bq_ok", 3)
                    need(act, "feat_ok", q * 2)
                    a.activation(ex[:, 0, :], p_qk[:, 0, :], ACT.Exp, bias=q_bias[:, :]).then_inc(s["exp_ok"], 1)
                    a.activation(ex[:, 1, :], p_qk[:, 1, :], ACT.Exp, bias=bcol[:, 1:2]).then_inc(s["exp_ok"], 1)
                    need(act, "v_ps", q + 1)
                    need(act, "rep_ps", (q - 1) * 4)
                    a.activation(vT[:, b, :], p_v, ACT.Identity, bias=bcol[:, 2:3]).then_inc(s["v_ok"], 1)
                if on(LE):
                    q, r = seq(i, u, LE), rset(u, LE)
                    j = TPS * ((u - LE) % BSEQ)
                    need(act, "log_ps", q + 1)
                    need(act, scat[r], turns(i, u, LE, UNROLL) * (16 * TOPK * BT))
                    a.activation(rows[:, r, j:j + TPS, 0:D], p_back, ACT.Copy).then_inc(s["rowh_ok"], 1)
                    need(act, "sc1_ok", turns(i, u, LE, BSEQ) - 1)
                    a.activation(rexp[:, r, j:j + TPS, :], p_log, ACT.Exp, scale=-1.0).then_inc(s["rexp_ok"], 1)
                if on(LB):
                    q = seq(i, u, LB)
                    need(act, "feat_ok", q * 2 + 2)
                    a.activation(lnk[:, :], feat[:, 1, :], ACT.Ln).then_inc(s["lnk_ok"], 1)
                    need(act, "lnk_ok", q + 1)
                    need(act, "rk_ok", q)
                    a.activation(rk0[:, :], lnk[:, :], ACT.Exp, scale=-1.0).then_inc(s["rk0_ok"], 1)

            part_a(act, step)

            def shared(i, u, on):
                if on(LH):
                    for m in range(SM):
                        n = item(i, u, LH) * SM + m
                        need(act, "sh_ps", n + 1)
                        need(act, "sh_gate", n - 1)
                        a.activation(act_s[:, m % 2, :], ps[:, m % 2, :], ACT.Silu).then_inc(s["sh_act"], 1)

            part_b(act, shared)

            def experts(i, u, on):
                if on(LT):
                    n, par = group(i, u, LT), u % 2
                    need(act, "xtT_ps", n + 1)
                    need(act, "hid_ps", n - 1)
                    a.activation(xtT[:, par, :], ps[:, 0, :], ACT.Copy).then_inc(s["xtT_ok"], 1)
                if on(LG):
                    n, par = group(i, u, LG), (u - LG) % 2
                    need(act, "hidT_ps", n + 1)
                    need(act, "y_ps", n - 1)
                    a.activation(hidT[:, par, :], ps[:, 1, :], ACT.Copy).then_inc(s["hidT_ok"], 1)
                if on(LHID):
                    n, par = group(i, u, LHID), (u - LHID) % 2
                    need(act, "hid_ps", n + 1)
                    need(act, "hidT_ps", n - 1)
                    a.activation(hid[:, par, :], ps[:, 2 + 2 * par, :], ACT.Silu).then_inc(s["hid_act"], 1)

            part_c(act, experts)

        @block.tensor
        def _(pe):
            mm = nc.tensor.matmul

            pe.wait_ge(s["ident_ok"], 2)
            pe.wait_ge(s["c_silu_ok"], 1)
            nc.tensor.transpose(ps[:, 0, 0:NSEQ], c_silu[:, :], ident[0:NSEQ, 0:NSEQ]).then_inc(s["cT_ps"], 1)
            pe.wait_ge(s["cT_ok"], 1)
            pe.wait_ge(s["w_mod"], 16)
            for k in range(6):
                m = mm(ps[:, 1, k * NSEQ:(k + 1) * NSEQ], wmod_sb[:, k * D:(k + 1) * D], cT[:, :],
                       start=True, stop=True)
            m.then_inc(s["mod_ps"], 1)
            for n in range(NSEQ // 4):
                need(pe, "gb_ok", n - 1)
                for k in range(4):
                    q = 4 * n + k
                    m = mm(ps[:, 2 + n % 2, k * D:(k + 1) * D], cT[:, q:q + 1].broadcast_to([D, P]),
                           wmod_sb[:, 5 * D:6 * D], start=True, stop=True)
                m.then_inc(s["gb_ps"], 1)
            pe.wait_ge(s["gb_ok"], NSEQ // 4)
            pe.wait_ge(s["mod_raw"], 1)
            pe.wait_ge(s["pick_ok"], 2)
            pe.wait_ge(s["sel_ok"], 3)
            pe.wait_ge(s["tri_ok"], 2)
            pe.wait_ge(s["consts_ok"], 7)

            def pair(q, b, n):
                need(pe, "v_ok", q + 1)
                need(pe, "scan_ok", q * (E + 1) + (2 * n - 1) if n >= 2 else (q - 1) * (E + 1) + (2 * n + 7))
                for j in range(2):
                    m = mm(p_rep[:, n % 2, j * L:(j + 1) * L], pick_f[:, 2 * n + j, :], vT[:, b, :],
                           start=True, stop=True)
                m.then_inc(s["rep_ps"], 1)

            def step(i, u, on):
                if on(LC):
                    pair(seq(i, u, LC), (u - LC) % 2, 0)
                if on(LD):
                    q = seq(i, u, LD)
                    need(pe, "rden_ok", q + 1)
                    need(pe, "rdT_ok", q)
                    for j in range(TPS):
                        for k in range(4):
                            m = mm(p_rdT[32 * k:32 * k + 32, j * P:(j + 1) * P], rden[:, j, :], ident[:, :],
                                   start=True, stop=True)
                    m.then_inc(s["rdT_ps"], 1)
                if on(LB):
                    q, b = seq(i, u, LB), (u - LB) % 2
                    need(pe, "xn1_ok", q * TPS + TPS)
                    need(pe, "v_ok", q)
                    for j in range(TPS):
                        m = nc.tensor.transpose(p_hT[:, j * P:(j + 1) * P], xn1[:, b, j, :], ident[:, :])
                    m.then_inc(s["hT_ps"], 1)
                if on(LC):
                    pair(seq(i, u, LC), (u - LC) % 2, 1)
                if on(LE):
                    q, b = seq(i, u, LE), (u - LE) % 2
                    need(pe, "xn2_ok", q * TPS + TPS)
                    need(pe, "h2_ok", q)
                    for j in range(TPS):
                        m = nc.tensor.transpose(p_h2T[:, j * P:(j + 1) * P], xn2[:, b, j, :], ident[:, :])
                    m.then_inc(s["h2T_ps"], 1)
                if on(LD):
                    q = seq(i, u, LD)
                    need(pe, "norm_ok", q + 1)
                    need(pe, "attT_ok", q)
                    if not isinstance(q, int) or q == 0:
                        need(pe, "w_attn", 16 * (E + 2))
                    for g in range(2):
                        m = mm(p_att, wout_sb[:, g, :], num[:, g, :], start=(g == 0), stop=(g == 1))
                    m.then_inc(s["att_ps"], 1)
                if on(LC):
                    pair(seq(i, u, LC), (u - LC) % 2, 2)
                if on(LB):
                    q, b = seq(i, u, LB), (u - LB) % 2
                    need(pe, "hT_ok", q + 1)
                    need(pe, "exp_ok", q * 2)
                    need(pe, "feat_ok", q * 2)
                    need(pe, "v_ok", q)
                    need(pe, "bq_ok", 3)
                    for k in range(2):
                        m = mm(p_qk[:, k, :], wqkv_sb[:, k * D:(k + 1) * D], hT[:, b, :], start=True, stop=True)
                    m.then_inc(s["qk_ps"], 1)
                    mm(p_v, wqkv_sb[:, 2 * D:3 * D], hT[:, b, :], start=True, stop=True).then_inc(s["v_ps"], 1)
                if on(LC):
                    pair(seq(i, u, LC), (u - LC) % 2, 3)
                if on(LE):
                    q, b = seq(i, u, LE), (u - LE) % 2
                    need(pe, "h2_ok", q + 1)
                    need(pe, "rexp_ok", q)
                    need(pe, "deneps_ok", min(q + 2, NSEQ) if isinstance(q, int) else q + 2)
                    if (u - LR2) % BSEQ == BSEQ - 1:
                        need(pe, "carry_ok", turns(i, u, LR2, BSEQ) + 1)
                    for j in range(TPS):
                        m = nc.tensor.transpose(p_back[:, j, :], h2[:, b, j * P:(j + 1) * P], ident[:, :])
                    for j in range(TPS):
                        m = mm(p_log[:, j, :], h2[:, b, j * P:(j + 1) * P], router_sb[:, :],
                               start=True, stop=True)
                    m.then_inc(s["log_ps"], 1)
                if on(LD):
                    q = seq(i, u, LD)
                    need(pe, "attT_ok", q + 1)
                    need(pe, "h2_ok", q)
                    for j in range(TPS):
                        m = nc.tensor.transpose(p_attb[:, j, :], attT[:, j * P:(j + 1) * P], ident[:, :])
                    m.then_inc(s["attb_ps"], 1)
                if on(LR1) and ends_batch(u, LR1):
                    n = batches(i, u, LR1)
                    need(pe, "chosen_ok", n)
                    need(pe, "carry_ok", n - 1)
                    if on(LE):
                        need(pe, "rexp_ok", seq(i, u, LE) + 1)
                    for j in range(BT):
                        mm(p_place[:, j, :], tri[:, :], chosen[:, j, :], start=True, stop=(j == 0))
                        for k in range(j):
                            mm(p_place[:, j, :], ones_bf[:, :], chosen[:, k, :], start=False, stop=(k == j - 1))
                    for j in range(BT):
                        m = mm(p_total, ones_bf[:, :], chosen[:, j, :], start=(j == 0), stop=(j == BT - 1))
                    m.then_inc(s["place_ps"], 1)
                if on(LC):
                    q, b = seq(i, u, LC), (u - LC) % 2
                    need(pe, "z_ok", q * (E + 1) + 1)
                    need(pe, "deneps_ok", q)
                    if on(LE):
                        need(pe, "rexp_ok", seq(i, u, LE) + 1)
                    for j in range(TPS):
                        m = mm(p_den[:, j, :], z[:, b, E, j * P:(j + 1) * P], head_sel[:, 0:H],
                               start=True, stop=True)
                    m.then_inc(s["den_ps"], 1)
                    need(pe, "norm_ok", q)
                    for g in range(2):
                        need(pe, "z_ok", q * (E + 1) + 5 + 4 * g)
                        for k in range(4):
                            m = mm(p_num[32 * k:32 * k + 32, g, :], head_sel[:, :], z[:, b, 4 * g + k, :],
                                   start=True, stop=True)
                    m.then_inc(s["num_ps"], 1)

            part_a(pe, step)

            pe.wait_ge(s["w_shared"], 48)
            for b in range(2):
                pe.wait_ge(copied[b], 16 * (NSEQ // 2))
            pe.wait_ge(s["scan_ok"], NSEQ * (E + 1))
            pe.wait_ge(s["norm_ok"], NSEQ)
            pe.wait_ge(s["feat_ok"], 2 * NSEQ)
            pe.wait_ge(s["v_ok"], NSEQ)

            def shared(i, u, on):
                if on(LH):
                    c0 = item(i, u, LH)
                    for m_ in range(SM):
                        n = c0 * SM + m_
                        need(pe, "sh_act", n - 1)
                        need(pe, "sh_gate", n - 1)
                        for w, bank in ((sw1_sb, 0), (sw2_sb, 2)):
                            m = mm(ps[:, bank + m_ % 2, :], w[:, m_ * P:(m_ + 1) * P],
                                   h2T[:, bass.ds(c0 * (FC * P), FC * P)], start=True, stop=True)
                        m.then_inc(s["sh_ps"], 1)
                if on(LO):
                    n, par = item(i, u, LO), (u - LO) % 2
                    need(pe, "sh_gate", n * SM + SM)
                    need(pe, "sh_mul", n - 1)
                    for j in range(FC):
                        for m_ in range(SM):
                            m = mm(ps[:, 4 + par, j * D:(j + 1) * D], gate_s[:, par, m_, j * P:(j + 1) * P],
                                   sw3_sb[:, m_, :], start=(m_ == 0), stop=(m_ == SM - 1))
                    m.then_inc(s["sh_out_ps"], 1)

            part_b(pe, shared)

            pe.wait_ge(s["w_routed"], 48)
            pe.wait_ge(s["tiles_ok"], 1)
            pe.wait_ge(s["sh_act"], NTILE // FC * SM)
            pe.wait_ge(s["sh_gate"], NTILE // FC * SM)
            pe.wait_ge(s["sh_mul"], NTILE // FC)

            def experts(i, u, on):
                if on(LT):
                    n, par = group(i, u, LT), u % 2
                    need(pe, xt_in[par], (i * (UNROLL_C // 2) + u // 2 + 1) * (16 * GT))
                    need(pe, "xtT_ok", n)
                    for j in range(GT):
                        m = nc.tensor.transpose(ps[:, 0, j * P:(j + 1) * P], xt[:, par, j, 0:D], ident[:, :])
                    m.then_inc(s["xtT_ps"], 1)
                if on(LG):
                    n, par = group(i, u, LG), (u - LG) % 2
                    need(pe, "hid_ok", n + 1)
                    need(pe, "hidT_ok", n)
                    for j in range(GT):
                        m = nc.tensor.transpose(ps[:, 1, j * P:(j + 1) * P], hid[:, par, j * P:(j + 1) * P],
                                                ident[:, :])
                    m.then_inc(s["hidT_ps"], 1)
                if on(LHID):
                    n, par = group(i, u, LHID), (u - LHID) % 2
                    experts_of = [pe.value_load(et_i[0:1, bass.ds(n * GT + j, 1)], min_val=0, max_val=NE - 1)
                                  for j in range(GT)]
                    need(pe, "xtT_ok", n + 1)
                    need(pe, "hid_act", n - 1)
                    need(pe, "hid_ok", n - 1)
                    for j in range(GT):
                        for w, bank in ((rw1_sb, 2), (rw2_sb, 3)):
                            m = mm(ps[:, bank + 2 * par, j * P:(j + 1) * P], xtT[:, par, j * P:(j + 1) * P],
                                   w[:, bass.ds(experts_of[j] * RH, RH)], start=True, stop=True)
                    m.then_inc(s["hid_ps"], 1)
                if on(LY):
                    n, par = group(i, u, LY), (u - LY) % 2
                    experts_of = [pe.value_load(et_i[0:1, bass.ds(n * GT + j, 1)], min_val=0, max_val=NE - 1)
                                  for j in range(GT)]
                    need(pe, "hidT_ok", n + 1)
                    need(pe, "y_ok", n - 1)
                    for j in range(GT):
                        m = mm(ps[:, 6 + par, j * D:(j + 1) * D], hidT[:, par, j * P:(j + 1) * P],
                               rw3_sb[:, bass.ds(experts_of[j] * D, D)], start=True, stop=True)
                    m.then_inc(s["y_ps"], 1)

            part_c(pe, experts)

        @block.vector
        def _(ve):
            v = nc.vector
            tt, ts, stt = v.tensor_tensor, v.tensor_scalar, v.scalar_tensor_tensor
            ve.wait_ge(s["c_exp_ok"], 1)
            ts(c_exp[:, :], c_exp[:, :], 1.0, None, ALU.add).then_inc(s["c_chain"], 1)
            ve.wait_ge(s["c_chain"], 1)
            v.reciprocal(c_exp[:, :], c_exp[:, :]).then_inc(s["c_chain"], 1)
            ve.wait_ge(s["c_chain"], 2)
            tt(c_silu[:, :], c_sb[:, :], c_exp[:, :], ALU.mult).then_inc(s["c_silu_ok"], 1)
            v.memset(ratio[:, :, 0:1], 0.0).then_inc(s["vconst_ok"], 1)
            v.memset(rden[:, :, :], 0.0).then_inc(s["vconst_ok"], 1)
            ve.wait_ge(s["bias_in"], 16 * 5)
            ve.wait_ge(s["w_attn"], 16 * (E + 2))
            ts(wqkv_sb[:, 0:D], wqkv_sb[:, 0:D], QSCALE, None, ALU.mult).then_inc(s["bq_ok"], 1)
            ts(q_bias[:, :], bcol[:, 0:1], QSCALE, None, ALU.mult).then_inc(s["bq_ok"], 1)
            ts(k_bias1[:, :], bcol[:, 1:2], 1.0 + EPS_FEAT, None, ALU.add).then_inc(s["bq_ok"], 1)
            ve.wait_ge(s["bq_ok"], 3)
            ts(q_bias1[:, :], q_bias[:, :], 1.0 + EPS_FEAT, None, ALU.add).then_inc(s["vconst_ok"], 1)
            ve.wait_ge(s["cT_ps"], 1)
            v.tensor_copy(cT[:, :], ps[:, 0, 0:NSEQ]).then_inc(s["cT_ok"], 1)
            ve.wait_ge(s["mod_ps"], 1)
            v.tensor_copy(mod[:, :, :], ps[:, 1, 0:6 * NSEQ].rearrange("p (k b) -> p k b", k=6)
                          ).then_inc(s["mod_raw"], 1)
            ve.wait_ge(s["mod_raw"], 1)
            done = 0
            for k in (1, 4):
                ts(mod[:, k, :], mod[:, k, :], 1.0, None, ALU.add).then_inc(s["mod_chain"], 1)
                done += 1

            def gate_of(dst, src, mag, sign, n, name):
                ts(mag, src, -1.0, None, ALU.mult).then_inc(s[name], 1)
                ts(sign, src, 0.0, 2.0, ALU.is_ge, ALU.mult).then_inc(s[name], 1)
                ve.wait_ge(s[name], n + 2)
                tt(mag, mag, src, ALU.max).then_inc(s[name], 1)
                ts(sign, sign, -1.0, None, ALU.add).then_inc(s[name], 1)
                ve.wait_ge(s[name], n + 4)
                ts(mag, mag, 0.25, None, ALU.max).then_inc(s[name], 1)
                ve.wait_ge(s[name], n + 5)
                return tt(dst, mag, sign, ALU.mult)

            gate_of(mod[:, 2, :], mod[:, 2, :], mod_abs[:, :], mod_sign[:, :], done, "mod_chain"
                    ).then_inc(s["mod_chain"], 1)
            ve.wait_ge(s["mod_chain"], done + 6)
            ts(ga_bout[:, :], mod[:, 2, :], bcol[:, 3:4], None, ALU.mult).then_inc(s["mod_ok"], 1)
            for n in range(NSEQ // 4):
                ve.wait_ge(s["gb_ps"], n + 1)
                raw = gb_rows[:, 4 * n:4 * n + 4, :]
                v.tensor_copy(raw, ps[:, 2 + n % 2, :].rearrange("p (k d) -> p k d", d=D)).then_inc(s["gb_ok"], 1)
                ve.wait_ge(s["gb_ok"], n + 1)
                gate_of(raw, raw, gb_abs[:, :, :], gb_sign[:, :, :], 6 * n, "gb_chain").then_inc(s["gb_chain"], 1)
            ve.wait_ge(s["consts_ok"], 7)
            v.tensor_copy(carry[:, :], expert_base[:, :]).then_inc(s["carry0_ok"], 1)
            ve.wait_ge(s["carry0_ok"], 1)
            ve.wait_ge(s["vconst_ok"], 3)

            def norm_stats(q, which, src, mv, var, names):
                st, ag, ep = names
                for j in range(TPS):
                    v.bn_stats(stats[:, which, j, :], src(j)).then_inc(s[st], 1)
                need_apart(ve, st, q * TPS + TPS)
                for j in range(TPS):
                    v.bn_aggr(mv[:, j, :], stats[:, which, j, :]).then_inc(s[ag], 1)
                need(ve, ag, q * TPS + TPS)
                ts(var[:, :], mv[:, :, 1:2].rearrange("p a b -> p (a b)"), EPS_LN, None, ALU.add).then_inc(s[ep], 1)

            def scan(q, b, f, data):
                v.tensor_tensor_scan(state[:, b, f, :], ratio[:, b, :], data, 0.0,
                                     ALU.mult, ALU.add).then_inc(s["scan_ok"], 1)

            def pair(q, b, n):
                need(ve, "rep_ps", q * 4 + n + 1)
                for j in range(2):
                    scan(q, b, 2 * n + j, p_rep[:, n % 2, j * L:(j + 1) * L])

            def step(i, u, on):
                if on(LC):
                    q, b = seq(i, u, LC), (u - LC) % 2
                    need(ve, "rk0_ok", q + 1)
                    tt(rkt[:, :], feat[:, 1, :], rk0[:, :], ALU.mult).then_inc(s["rkt_ok"], 1)
                    need(ve, "rkt_ok", q + 1)
                    stt(out=rk[:, :], in0=rkt[:, :], scalar=2.0, in1=rk0[:, :], op0=ALU.subtract,
                        op1=ALU.mult).then_inc(s["rk_ok"], 1)
                if on(LD):
                    q = seq(i, u, LD)
                    need(ve, "den_ps", q + 1)
                    ts(den[:, :, :], p_den, EPS_DEN, None, ALU.add).then_inc(s["deneps_ok"], 1)
                if on(LC):
                    need(ve, "rk_ok", q_c(i, u) + 1)
                    stt(out=ratio[:, (u - LC) % 2, 1:L], in0=feat[:, 1, 0:L - 1], scalar=-1.0, in1=rk[:, 1:L],
                        op0=ALU.mult, op1=ALU.mult).then_inc(s["ratio_ok"], 1)
                if on(LD):
                    q = seq(i, u, LD)
                    need(ve, "deneps_ok", q + 1)
                    need(ve, "rdT_ps", q)
                    v.reciprocal(rden[:, :, 0:H], den[:, :, :]).then_inc(s["rden_ok"], 1)
                if on(LR2) and ends_batch(u, LR2):
                    places(i, u)
                if on(LC):
                    q, b = seq(i, u, LC), (u - LC) % 2
                    need(ve, "ratio_ok", q + 1)
                    need(ve, "z_ok", (q - 1) * (E + 1))
                    scan(q, b, E, ones[:, :])
                    pair(q, b, 0)
                if on(LD):
                    q = seq(i, u, LD)
                    need(ve, "num_ps", q + 1)
                    need(ve, "rdT_ok", q + 1)
                    need(ve, "att_ps", q)
                    tt(num[:, :, :], p_num, spread(rdenT[:, :], 1, 2), ALU.mult).then_inc(s["norm_ok"], 1)
                if on(LE):
                    q, b = seq(i, u, LE), (u - LE) % 2
                    need(ve, "rstd2_ok", q + 1)
                    need(ve, "h2T_ps", q - 1)
                    for j in range(TPS):
                        ts(xn2[:, b, j, :], resid[:, bass.ds(q * TPS + j, 1), :].rearrange("p a d -> p (a d)"),
                           mv2[:, j, 0:1], rstd2[:, j:j + 1], ALU.subtract, ALU.mult).then_inc(s["xn2_ok"], 1)
                if on(LC):
                    pair(seq(i, u, LC), (u - LC) % 2, 1)
                if on(LA):
                    q = seq(i, u, LA)
                    need_apart(ve, x_in[u % 2], turns(i, u, LA, 2) * 16 + 16)
                    norm_stats(q, 0, lambda j: resid[:, bass.ds(q * TPS + j, 1), :].rearrange("p a d -> p (a d)"),
                               mv1, var1, ("stats1", "aggr1", "veps1"))
                if on(LC):
                    pair(seq(i, u, LC), (u - LC) % 2, 2)
                if on(LB):
                    q = seq(i, u, LB)
                    need(ve, "exp_ok", q * 2 + 2)
                    ts(ex[:, :, :], ex[:, :, :], 1.0, EPS_FEAT, ALU.min, ALU.add).then_inc(s["exmin_ok"], 1)
                if on(LA):
                    q, b = seq(i, u, LA), u % 2
                    need(ve, "rstd1_ok", q + 1)
                    need(ve, "hT_ps", q - 1)
                    for j in range(TPS):
                        ts(xn1[:, b, j, :], resid[:, bass.ds(q * TPS + j, 1), :].rearrange("p a d -> p (a d)"),
                           mv1[:, j, 0:1], rstd1[:, j:j + 1], ALU.subtract, ALU.mult).then_inc(s["xn1_ok"], 1)
                if on(LB):
                    q, b = seq(i, u, LB), (u - LB) % 2
                    need(ve, "exmin_ok", q + 1)
                    for k, bias in ((0, q_bias1), (1, k_bias1)):
                        stt(out=feat[:, k, :], in0=p_qk[:, k, :], scalar=bias[:, :], in1=ex[:, k, :],
                            op0=ALU.add, op1=ALU.max).then_inc(s["feat_ok"], 1)
                if on(LD):
                    q = seq(i, u, LD)
                    need(ve, "attb_ps", q + 1)
                    tt(resid[:, bass.ds(q * TPS, TPS), :], resid[:, bass.ds(q * TPS, TPS), :], p_attb,
                       ALU.add).then_inc(s["x1_ok"], 1)
                if on(LB):
                    q, b = seq(i, u, LB), (u - LB) % 2
                    need(ve, "feat_ok", q * 2 + 2)
                    need(ve, "z_ok", (q - 1) * (E + 1))
                    tt(qk[:, b, :], feat[:, 0, :], feat[:, 1, :], ALU.mult).then_inc(s["qk_ok"], 1)
                if on(LD):
                    q = seq(i, u, LD)
                    need_apart(ve, "x1_ok", q + 1)
                    norm_stats(q, 1, lambda j: resid[:, bass.ds(q * TPS + j, 1), :].rearrange("p a d -> p (a d)"),
                               mv2, var2, ("stats2", "aggr2", "veps2"))
                if on(LC):
                    pair(seq(i, u, LC), (u - LC) % 2, 3)
                if on(LR1) and ends_batch(u, LR1):
                    top2(i, u)

            def q_c(i, u):
                return seq(i, u, LC)

            def top2(i, u):
                r, n = rset(u, LR1), batches(i, u, LR1)
                need(ve, "rexp_ok", n * BSEQ)
                ts(score1[:, :, :], rexp[:, r, :, :], 1.0, None, ALU.add).then_inc(s["sc1_ok"], 1)
                need(ve, "sc1_ok", n)
                v.reciprocal(score[:, :, :], score1[:, :, :]).then_inc(s["sc_ok"], 1)
                need(ve, "sc_ok", n)
                tt(sel[:, :, :], score[:, :, :], spread(bias_rows[:, :], 1, BT), ALU.add).then_inc(s["selb_ok"], 1)
                need_apart(ve, "selb_ok", n)
                for j in range(BT):
                    v.max(top[:, j, :], sel[:, j, :]).then_inc(s["top_ok"], 1)
                need_apart(ve, "top_ok", n * BT)
                for j in range(BT):
                    v.max_index(topi[:, j, :], top[:, j, :], sel[:, j, :]).then_inc(s["topi_ok"], 1)
                need(ve, "topi_ok", n * BT)
                v.tensor_copy(topf[:, :, :], topi[:, :, 0:TOPK]).then_inc(s["topf_ok"], 1)
                need(ve, "topf_ok", n)
                for k in range(TOPK):
                    tt(onehot[:, k, :, :], spread(eio[:, :], 1, BT),
                       topf[:, :, k:k + 1].broadcast_to([P, BT, NE]), ALU.is_equal).then_inc(s["onehot_ok"], 1)
                need(ve, "onehot_ok", n * TOPK)
                tt(chosen[:, :, :], onehot[:, 0, :, :], onehot[:, 1, :, :], ALU.add).then_inc(s["chosen_ok"], 1)
                tt(gtmp[:, :, :, :], onehot[:, :, :, :], spread(score[:, :, :], 1, TOPK),
                   ALU.mult).then_inc(s["gtmp_ok"], 1)
                v.tensor_copy(rows[:, r, :, C_E1:C_E1 + 1], topf[:, :, 0:1]).then_inc(s["rowmeta_ok"], 1)
                v.tensor_copy(rows[:, r, :, C_ID:C_ID + 1],
                              tok_id[:, bass.ds(n * BT - BT, BT)].unsqueeze(2)).then_inc(s["rowmeta_ok"], 1)
                need(ve, "gtmp_ok", n)
                v.tensor_reduce(rows[:, r, :, C_G1:C_G2 + 1].rearrange("p j k -> p k j"), gtmp[:, :, :, :],
                                AX_X, ALU.add).then_inc(s["rowmeta_ok"], 1)

            def places(i, u):
                r, n = rset(u, LR2), batches(i, u, LR2)
                need(ve, "place_ps", n)
                need(ve, "carry_ok", n - 1)
                tt(place[:, :, :], p_place, spread(carry[:, :], 1, BT), ALU.add).then_inc(s["place_ok"], 1)
                need(ve, "place_ok", n)
                tt(ptmp[:, :, :, :], onehot[:, :, :, :], spread(place[:, :, :], 1, TOPK),
                   ALU.mult).then_inc(s["ptmp_ok"], 1)
                tt(carry[:, :], carry[:, :], p_total, ALU.add).then_inc(s["carry_ok"], 1)
                need(ve, "ptmp_ok", n)
                with nc.allow_low_precision(reason="whole numbers below 2^24, one term not zero"):
                    v.tensor_reduce(pos[:, r, :, :], ptmp[:, :, :, :], AX_X, ALU.add).then_inc(s["pos_ok"], 1)

            part_a(ve, step)

            links = [0]

            def link(ins):
                links[0] += 1
                ins.then_inc(s["tb"], 1)
                ve.wait_ge(s["tb"], links[0])

            ve.wait_ge(s["carry_ok"], NSEQ // BSEQ)
            link(tt(cnt[:, :], carry[:, :], expert_base[:, :], ALU.subtract))
            v.tensor_copy(cnt_i[:, :], cnt[:, :]).then_inc(s["cnt_ok"], 1)
            link(ts(nt_f[:, :], cnt[:, :], 1.0 / P, (P - 1.0) / P - (P - 1.0) / (2 * P), ALU.mult, ALU.add))
            link(v.tensor_copy(nt_i[:, :], nt_f[:, :]))
            link(v.tensor_copy(nt[:, :], nt_i[:, :]))
            link(v.tensor_tensor_scan(end[:, :], ones[:, 0:NE], nt[:, :], 0.0, ALU.mult, ALU.add))
            link(tt(offt[:, 0:NE], end[:, :], nt[:, :], ALU.subtract))
            link(stt(out=off[:, 0:NE], in0=offt[:, 0:NE], scalar=-float(P), in1=expert_base[:, :],
                     op0=ALU.mult, op1=ALU.add))
            link(ts(off[:, NE:NE + 1], end[:, NE - 1:NE], -float(P), float(SURPLUS), ALU.mult, ALU.add))
            link(tt(doff[:, :], off[:, 1:NE + 1], off[:, 0:NE], ALU.subtract))
            link(tt(past[:, :, :], jio[:, :].unsqueeze(2).broadcast_to([P, RT, NE]), spread(end[:, :], 1, RT),
                    ALU.is_ge))
            link(v.tensor_reduce(et[:, :], past[:, :, :], AX_X, ALU.add))
            link(ts(etw[:, :], et[:, :], NE - 1.0, None, ALU.min))
            link(v.tensor_copy(et_i[:, :], etw[:, :]))
            link(tt(past[:, :, :], past[:, :, :], spread(doff[:, :], 1, RT), ALU.mult))
            link(v.tensor_reduce(row0[:, :], past[:, :, :], AX_X, ALU.add))
            link(stt(out=row0b[:, :], in0=jio[:, :], scalar=float(P), in1=row0[:, :], op0=ALU.mult, op1=ALU.add))
            link(ts(row0[:, :], row0b[:, :], off[:, 0:1], None, ALU.add))
            v.tensor_copy(row0_i[:, :], row0[:, :]).then_inc(s["tiles_ok"], 1)
            ve.wait_ge(s["gb_chain"], 6 * (NSEQ // 4))

            def shared(i, u, on):
                if on(LH):
                    par = u % 2
                    need(ve, "sh_out_ps", item(i, u, LH) - 1)
                    for m in range(SM):
                        n = item(i, u, LH) * SM + m
                        need(ve, "sh_act", n + 1)
                        need(ve, "sh_ps", n + 1)
                        tt(gate_s[:, par, m, :], act_s[:, m % 2, :], ps[:, 2 + m % 2, :],
                           ALU.mult).then_inc(s["sh_gate"], 1)
                if on(LO):
                    n, par = item(i, u, LO), (u - LO) % 2
                    need(ve, "sh_out_ps", n + 1)
                    need(ve, "sh_mul", n)
                    for k in range(2):
                        gb = gb_rows[:, bass.ds(n * 2 + k, 1), :].broadcast_to([P, TPS, D])
                        tt(sh_mul[:, k * TPS:(k + 1) * TPS, :],
                           ps[:, 4 + par, k * L:(k + 1) * L].rearrange("p (a d) -> p a d", d=D), gb,
                           ALU.mult).then_inc(s["sh_half"], 1)
                    need(ve, "sh_half", n * 2 + 2)
                    tt(resid[:, bass.ds(n * FC, FC), :], resid[:, bass.ds(n * FC, FC), :], sh_mul[:, :, :],
                       ALU.add).then_inc(s["sh_mul"], 1)

            part_b(ve, shared)

            def experts(i, u, on):
                if on(LHID):
                    n, par = group(i, u, LHID), (u - LHID) % 2
                    need(ve, "hid_act", n + 1)
                    need(ve, "hid_ps", n + 1)
                    tt(hid[:, par, :], hid[:, par, :], ps[:, 3 + 2 * par, :], ALU.mult).then_inc(s["hid_ok"], 1)
                    quad = (u - LHID) % UNROLL_C
                    e1, id2, g1, g2 = (xt[:, par, :, k:k + 1].rearrange("p j a -> p (j a)")
                                       for k in (C_E1, C_ID, C_G1, C_G2))
                    half = i * (UNROLL_C // 2) + (u - LHID) // 2
                    need(ve, xt_in[par], (half + 1) * (16 * GT))
                    need(ve, "gate_ok", n)
                    need(ve, "dest_ok", n)
                    tt(first[:, :], e1, et[:, bass.ds(n * GT, GT)], ALU.is_equal).then_inc(s["first_ok"], 1)
                    tt(gdiff[:, :], g1, g2, ALU.subtract).then_inc(s["gdiff_ok"], 1)
                    need(ve, "first_ok", n + 1)
                    need(ve, "gdiff_ok", n + 1)
                    tt(gsel[:, :], first[:, :], gdiff[:, :], ALU.mult).then_inc(s["gsel_ok"], 1)
                    need(ve, yout[par], (half - 1) * (16 * GT))
                    stt(out=dest[:, quad, :], in0=first[:, :], scalar=-float(NTOK), in1=id2,
                        op0=ALU.mult, op1=ALU.add).then_inc(s["dest_ok"], 1)
                    need(ve, "gsel_ok", n + 1)
                    need(ve, "y_ok", n - 3)
                    tt(gate[:, quad, :], gsel[:, :], g2, ALU.add).then_inc(s["gate_ok"], 1)
                if on(LY):
                    n, par = group(i, u, LY), (u - LY) % 2
                    need(ve, "y_ps", n + 1)
                    need(ve, yout[par], (i * (UNROLL_C // 2) + (u - LY) // 2) * (16 * GT))
                    tt(yrow[:, par, :, :], ps[:, 6 + par, :].rearrange("p (j d) -> p j d", d=D),
                       gate[:, (u - LY) % UNROLL_C, :].unsqueeze(2).broadcast_to([P, GT, D]), ALU.mult).then_inc(s["y_ok"], 1)

            ve.wait_ge(s["sh_mul"], NTILE // FC)
            part_c(ve, experts)

            def total(n, i, par):
                need(ve, y_in[par], i * 32 + 32)
                need(ve, o_out[par], i * 16)
                tt(osum[:, par, :, :], y0[:, par, :, :], y1[:, par, :, :], ALU.add).then_inc(s["osum0"], 1)
                need(ve, "osum0", n + 1)
                for k in range(2):
                    gb = gb_rows[:, bass.ds(n * 2 + k, 1), :].broadcast_to([P, TPS, D])
                    tt(osum[:, par, k * TPS:(k + 1) * TPS, :], osum[:, par, k * TPS:(k + 1) * TPS, :], gb,
                       ALU.mult).then_inc(s["osum1"], 1)
                need(ve, "osum1", n * 2 + 2)
                tt(osum[:, par, :, :], osum[:, par, :, :], resid[:, bass.ds(n * FC, FC), :],
                   ALU.add).then_inc(s["osum_ok"], 1)

            for par in range(2):
                total(par, 0, par)
            with ve.Fori(1, NTILE // FC // 2, 1) as i:
                for par in range(2):
                    total(i * 2 + par, i, par)


_INS = ["L0_attn_x", "L0_attn_W_qkv", "L0_attn_b_qkv", "L0_attn_W_out", "L0_attn_b_out", "L0_ffn_router_w",
        "L0_ffn_expert_bias", "L0_ffn_shared_w1", "L0_ffn_shared_w2", "L0_ffn_shared_w3", "L0_ffn_routed_w1",
        "L0_ffn_routed_w2", "L0_ffn_routed_w3", "L0_c", "L0_wmod"]


def kernel(**inputs):
    import numpy as np
    import concourse.bacc as bacc
    from concourse.bass_utils import run_bass_kernel_spmd

    nc = bacc.Bacc("TRN2", target_bir_lowering=False, num_devices=1)
    arrays, args = {}, []
    for name in _INS:
        a = np.ascontiguousarray(inputs[name])
        arrays[f"in_{name}"] = a
        args.append(nc.dram_tensor(f"in_{name}", a.shape, mybir.dt.from_np(a.dtype), kind="ExternalInput").ap())
    args.append(nc.dram_tensor("out_x", (NSEQ, L, D), F32, kind="ExternalOutput").ap())
    adaln_block(nc, *args)
    result = run_bass_kernel_spmd(nc, [arrays], core_ids=[0])
    return result.results[0]["out_x"]
```

```python
from contextlib import ExitStack

import concourse.bass as bass
from concourse import mybir

F32 = mybir.dt.float32
BF16 = mybir.dt.bfloat16
U32 = mybir.dt.uint32
I32 = mybir.dt.int32
ALU = mybir.AluOpType
ACT = mybir.ActivationFunctionType
AX_X = mybir.AxisListType.X

P = 128
D = 128
NSEQ, L = 32, 256
TPS = L // P
NTILE = NSEQ * TPS
NTOK = NSEQ * L
H, E = 16, 8
NE, RH, TOPK = 16, 128, 2
SH = 512
SM = SH // P
EPS_FEAT, EPS_DEN, EPS_LN = 1e-4, 1e-6, 1e-5
QSCALE = float(E) ** -0.5

UNROLL = 4
ROW = D + 4
C_ID, C_E1, C_G1, C_G2 = D, D + 1, D + 2, D + 3
CAP = NTOK + P
SURPLUS = NE * CAP
RT = NTOK * TOPK // P + NE
GT = 4
UNROLL_C = 4
NG = RT // GT
CB = 8
YROWS = NTOK * TOPK + 2 * NE * P
UD = 4
FC = 4
NB = NTILE // FC - CB


def adaln_block(nc, x, w_qkv, b_qkv, w_out, b_out, router_w, expert_bias,
                sw1, sw2, sw3, rw1, rw2, rw3, c, wmod, out):
    with ExitStack() as ctx:
        def sb(name, shape, dt=F32):
            return ctx.enter_context(nc.sbuf_tensor(name, shape, dt))

        def sem(name):
            return ctx.enter_context(nc.semaphore(name))

        lists = nc.dram_tensor("lists", [SURPLUS + NE * P, ROW], F32, kind="Internal").ap()
        routed = nc.dram_tensor("routed", [YROWS, D], F32, kind="Internal").ap()

        resid = sb("resid", [P, NTILE, D])
        h2T = sb("h2T", [D, NTOK])
        gb_rows = sb("gb_rows", [P, NSEQ, D])
        wqkv_sb = sb("wqkv_sb", [D, 3 * D])
        wout_sb = sb("wout_sb", [P, 2, D])
        wmod_sb = h2T[:, 0:6 * D]
        router_sb = sb("router_sb", [D, NE])
        bias_rows = sb("bias_rows", [P, NE])
        sw1_sb = sb("sw1_sb", [D, SH])
        sw2_sb = sb("sw2_sb", [D, SH])
        sw3_sb = sb("sw3_sb", [P, SM, D])
        rw1_sb = sb("rw1_sb", [D, NE * RH])
        rw2_sb = sb("rw2_sb", [D, NE * RH])
        rw3_sb = sb("rw3_sb", [RH, NE * D])
        ident = sb("ident", [P, P])
        pick_f = sb("pick_f", [P, E, P])
        head_sel = sb("head_sel", [P, 32])
        tri = sb("tri", [P, P], BF16)
        ones_bf = sb("ones_bf", [P, P], BF16)
        ones = sb("ones", [P, L])
        eio = sb("eio", [P, NE])
        expert_base = sb("expert_base", [P, NE])
        tok_id = sb("tok_id", [P, NTILE])
        fill = sb("fill", [P, NE, ROW])
        c_sb = sb("c_sb", [NSEQ, D])
        c_exp = sb("c_exp", [NSEQ, D])
        c_silu = sb("c_silu", [NSEQ, D])
        cT = sb("cT", [D, NSEQ])
        mod = sb("mod", [D, 6, NSEQ])
        mod_abs = sb("mod_abs", [D, NSEQ])
        mod_sign = sb("mod_sign", [D, NSEQ])
        mod_abs2 = sb("mod_abs2", [D, NSEQ])
        mod_sign2 = sb("mod_sign2", [D, NSEQ])
        ga_bout = sb("ga_bout", [D, NSEQ])
        bcol = sb("bcol", [P, 4])
        q_bias = sb("q_bias", [P, 1])
        q_bias1 = sb("q_bias1", [P, 1])
        k_bias1 = sb("k_bias1", [P, 1])
        pool_note = sb("pool_note", [1, 1])
        carrier_dve = sb("carrier_dve", [1, 6])
        carrier_pool = sb("carrier_pool", [1, 1])
        stats = sb("stats", [P, 2, TPS, 6])
        mv = sb("mv", [P, 2, TPS, 2])
        var = sb("var", [P, 2, TPS])
        lnvar = sb("lnvar", [P, 2, TPS])
        rguess = sb("rguess", [P, 2, TPS])
        rstep1 = sb("rstep1", [P, 2, TPS])
        rstep2 = sb("rstep2", [P, 2, TPS])
        rstd = sb("rstd", [P, 2, TPS])
        shift = sb("shift", [P, 2, TPS])
        pairs_a = sb("pairs_a", [P, 6, 2, L])
        xn1 = pairs_a[:, 0, :, :].rearrange("p b (a d) -> p b a d", a=TPS)
        xn2 = pairs_a[:, 1, :, :].rearrange("p b (a d) -> p b a d", a=TPS)
        hT = pairs_a[:, 2, :, :]
        singles_a = sb("singles_a", [P, 10, L])
        ex = singles_a[:, 0:2, :]
        feat = singles_a[:, 2:4, :]
        qk = pairs_a[:, 3, :, :]
        lnk = singles_a[:, 4, :]
        rk0 = singles_a[:, 5, :]
        rkt = singles_a[:, 6, :]
        rk = singles_a[:, 7, :]
        ratio = pairs_a[:, 4, :, :]
        vT = pairs_a[:, 5, :, :]
        state = sb("state", [P, 2, E + 1, L])
        z = sb("z", [P, 2, E + 1, L])
        rden = sb("rden", [P, TPS, 32])
        den = sb("den", [P, TPS, H])
        rdenT = sb("rdenT", [P, L])
        num = singles_a[:, 8:10, :]
        attT = sb("attT", [D, L])
        h2 = sb("h2", [D, 2, L])
        rows = sb("rows", [P, UNROLL, TPS, ROW])
        rexp = sb("rexp", [P, 2, TPS, NE])
        score1 = sb("score1", [P, TPS, NE])
        score = sb("score", [P, TPS, NE])
        sel = sb("sel", [P, TPS, NE])
        top = sb("top", [P, TPS, 8])
        topi = sb("topi", [P, TPS, 8], U32)
        topf = sb("topf", [P, TOPK, TPS])
        onehot = sb("onehot", [P, TOPK, TPS, NE])
        chosen = sb("chosen", [P, TPS, NE], BF16)
        gtmp = sb("gtmp", [P, TOPK, TPS, NE])
        carry = sb("carry", [P, NE])
        place = sb("place", [P, TPS, NE])
        ptmp = sb("ptmp", [P, TOPK, TPS, NE])
        pos = sb("pos", [P, UNROLL, TOPK, TPS], U32)
        cnt = sb("cnt", [P, NE])
        cnt_i = sb("cnt_i", [P, NE], I32)
        nt_f = sb("nt_f", [P, NE])
        nt_i = sb("nt_i", [P, NE], I32)
        nt = sb("nt", [P, NE])
        end = sb("end", [P, NE])
        off = sb("off", [P, NE + 1])
        offt = sb("offt", [P, NE + 1])
        doff = sb("doff", [P, NE])
        jio = sb("jio", [P, RT])
        past = singles_a[:, :, :].rearrange("p a l -> p (a l)")[:, 0:RT * NE].rearrange(
            "p (j e) -> p j e", e=NE)
        et = sb("et", [P, RT])
        etw = sb("etw", [P, RT])
        row0 = sb("row0", [P, RT])
        row0b = sb("row0b", [P, RT])
        packed_f = sb("packed_f", [P, NG])
        group_experts = sb("group_experts", [P, NG], I32)
        row0_i = sb("row0_i", [P, RT], I32)
        a_state = state[:, :, :, :].rearrange("p a f l -> p (a f l)")
        a_z = z[:, :, :, :].rearrange("p a f l -> p (a f l)")
        W = FC * P
        gate_s = a_state[:, 0:2 * SM * W].rearrange("p (b m t) -> p b m t", b=2, m=SM)
        act_s = a_z[:, 0:2 * W].rearrange("p (b t) -> p b t", b=2)
        xtT = a_z[:, 2 * W:4 * W].rearrange("p (b t) -> p b t", b=2)
        hid = a_z[:, 4 * W:6 * W].rearrange("p (b t) -> p b t", b=2)
        a_pairs = pairs_a[:, :, :, :].rearrange("p a b l -> p (a b l)")
        hidT = a_z[:, 6 * W:8 * W].rearrange("p (b t) -> p b t", b=2)
        xt = a_pairs[:, 0:UNROLL_C * GT * ROW].rearrange("p (b j r) -> p b j r", b=UNROLL_C, r=ROW)
        yrow = [w[:, 8 * W:9 * W].rearrange("p (j d) -> p j d", d=D) for w in (a_state, a_z)]
        sh_mul = sb("sh_mul", [P, FC, D])
        first = sb("first", [P, GT])
        gdiff = sb("gdiff", [P, GT])
        gsel = sb("gsel", [P, GT])
        gate = sb("gate", [P, UNROLL_C, GT])
        dest = sb("dest", [P, UNROLL_C, GT], U32)
        y0, y1, osum = (w[:, 0:UD * W].rearrange("p (b a d) -> p b a d", b=UD, d=D)
                        for w in (rw1_sb, rw2_sb, rw3_sb))

        ps = ctx.enter_context(nc.psum_tensor("ps", [P, 8, 512], F32))
        p_hT = ps[:, 0, 0:L]
        p_v = ps[:, 0, L:2 * L]
        p_qk = ps[:, 1, :].rearrange("p (a l) -> p a l", a=2)
        p_rep = ps[:, 2:4, :]
        p_num = ps[:, 4, :].rearrange("p (a l) -> p a l", a=2)
        p_rdT = ps[:, 5, 0:L]
        p_att = ps[:, 5, L:2 * L]
        p_attb = ps[:, 6, 0:L].rearrange("p (a d) -> p a d", a=TPS)
        p_h2T = ps[:, 6, L:2 * L]
        p_back = ps[:, 7, 0:L].rearrange("p (a d) -> p a d", a=TPS)
        p_den = ps[:, 7, L:L + TPS * H].rearrange("p (a h) -> p a h", a=TPS)
        p_log = ps[:, 7, 288:288 + TPS * NE].rearrange("p (a e) -> p a e", a=TPS)
        p_place = ps[:, 7, 320:320 + TPS * NE].rearrange("p (a e) -> p a e", a=TPS)
        p_total = ps[:, 7, 448:448 + NE]

        names = """w_attn w_mod w_shared w_routed bias_in c_in fill_ok ident_ok pick_ok sel_ok tri_ok
            consts_ok fill_zero fill_cols vconst_ok c_exp_ok c_chain c_silu_ok cT_ps cT_ok mod_ps mod_raw mod_ok
            mod_chain gb_ready gb_ps gb_ok gb_chain bq_ok wout_zero surplus_out carry0_ok
            stats1 aggr1 veps1 lnvar_ok rguess_ok rstep1_ok rstep2_ok rstd_ok shift_ok xn1_ok hT_ps hT_ok qk_ps v_ps exp_ok v_ok exmin_ok feat_ok qk_ok lnk_ok
            rk0_ok rkt_ok rk_ok ratio_ok rep_ps scan_ok z_ok den_ps deneps_ok rden_ok rdT_ps rdT_ok num_ps norm_ok
            att_ps attT_ok attb_ps x1_ok stats2 aggr2 veps2 xn2_ok h2T_ps h2_ok log_ps
            rowh_ok rexp_ok sc1_ok sc_ok selb_ok top_ok topi_ok topf_ok onehot_ok chosen_ok gtmp_ok rowmeta_ok
            place_ps place_ok ptmp_ok pos_ok carry_ok
            tb cnt_ok tiles_ok fills_out sh_ps sh_act sh_gate sh_out_ps sh_half sh_mul
            xtT_ps xtT_ok hidT_ps hidT_ok hid_ps hid_act hid_ok y_ps y_ok first_ok gdiff_ok gsel_ok gate_ok dest_ok
            osum0 osum1 osum_ok carrier_a carrier_c""".split()
        s = {n: sem(n) for n in names}
        x_in = [sem(f"x_in{i}") for i in range(2)]
        copied = [sem(f"h2_copied{i}") for i in range(2)]
        scat = [sem(f"scattered{i}") for i in range(UNROLL)]
        xt_in = [sem(f"xt_in{i}") for i in range(UNROLL_C)]
        yout = [sem(f"y_scattered{i}") for i in range(2)]
        y_in = [sem(f"y_in{i}") for i in range(UD)]
        o_out = [sem(f"out_written{i}") for i in range(UD)]

        def need(eng, name, n):
            if not isinstance(n, int) or n > 0:
                eng.wait_ge(s[name] if isinstance(name, str) else name, n)

        def need_apart(eng, name, n, place_of="x_in stats1 stats2 x1_ok selb_ok top_ok".split()):
            need(eng, name, n)
            if not isinstance(n, int):
                k = place_of.index(name) if isinstance(name, str) else 0
                nc.vector.memset(carrier_dve[:, k:k + 1], 0.0)

        def need_apart_pool(eng, name, n, written, times):
            need(eng, written, times)
            need(eng, name, n)
            nc.gpsimd.tensor_tensor(carrier_pool[:, :], eio[0:1, 0:1], eio[0:1, 0:1],
                                    ALU.add).then_inc(s[written], 1)

        LA, LB, LC, LD, LE, LR1, LR2 = 0, 1, 2, 3, 4, 5, 6
        LH, LO = 0, 1
        LT, LHID, LG, LY = 0, 1, 2, 3
        LX, LCOPY = 0, 7

        def pipeline(eng, step, count, unroll, lags, head, looped=None):
            looped = looped or count
            def written_out(t):
                step(t // unroll, t % unroll, lambda lag: 0 <= t - lag < count)
            for t in range(head):
                written_out(t)
            with eng.Fori(head // unroll, looped // unroll, 1) as i:
                for u in range(unroll):
                    step(i, u, lambda lag: True)
            for t in range(looped, count + lags):
                written_out(t)

        def part_a(eng, step, lags=LR2, head=2 * UNROLL):
            pipeline(eng, step, NSEQ, UNROLL, lags, head)

        def part_b(eng, step):
            pipeline(eng, step, NB, 2, LO, 4)

        def part_c(eng, step):
            pipeline(eng, step, NG, UNROLL_C, LY, 2 * UNROLL_C, UNROLL_C * CB)

        def shares(i):
            return not isinstance(i, int) or i < CB

        def puts_out(i, u):
            return u == 0 and (not isinstance(i, int) or 1 <= i <= CB)

        def seq(i, u, lag):
            return i * UNROLL + (u - lag)

        def item(i, u, lag):
            return i * 2 + (u - lag)

        def group(i, u, lag):
            return i * UNROLL_C + (u - lag)

        def turns(i, u, lag, every):
            return i * (UNROLL // every) + (u - lag) // every

        def cap(n, most):
            return min(n, most) if isinstance(n, int) else n

        def rset(u, lag):
            return (u - lag) % UNROLL

        def spread(ap, axis, n):
            shape = list(ap.shape)
            return ap.unsqueeze(axis).broadcast_to(shape[:axis] + [n] + shape[axis:])

        block = ctx.enter_context(nc.Block())

        @block.sync
        def _(sp):
            sp.dma_start(c_sb[:, :], c).then_inc(s["c_in"], 16)
            for i in range(2):
                sp.dma_start(resid[:, TPS * i:TPS * i + TPS, :],
                             x[i].rearrange("(a p) d -> p a d", p=P)).then_inc(x_in[i], 16)
            sp.dma_start(wmod_sb[:, :], wmod).then_inc(s["w_mod"], 16)
            sp.dma_start(wqkv_sb[:, :], w_qkv).then_inc(s["w_attn"], 16)
            for i in range(3):
                sp.dma_start(bcol[:, i:i + 1],
                             b_qkv[i * D:(i + 1) * D].rearrange("(p a) -> p a", a=1)).then_inc(s["bias_in"], 16)
            sp.dma_start(bcol[:, 3:4], b_out.rearrange("(p a) -> p a", a=1)).then_inc(s["bias_in"], 16)
            sp.dma_start(bias_rows[:, :], expert_bias.partition_broadcast(P)).then_inc(s["bias_in"], 16)
            sp.wait_ge(s["wout_zero"], 1)
            for f in range(E):
                sp.dma_start(wout_sb[32 * (f % 4):32 * (f % 4) + H, f // 4, :],
                             w_out.rearrange("(h f) d -> f h d", f=E)[f]).then_inc(s["w_attn"], 16)
            sp.dma_start(router_sb[:, :], router_w).then_inc(s["w_attn"], 16)

            sp.wait_ge(s["fill_ok"], 1)
            sp.dma_start(lists[SURPLUS:SURPLUS + NE * P, :].rearrange("(p e) r -> p e r", p=P),
                         fill[:, :, :]).then_inc(s["surplus_out"], 16)

            def step(i, u, on):
                if on(LX) and not (isinstance(i, int) and i == 0 and u < 2):
                    n = turns(i, u, LX, 2)
                    need(sp, x_in[u % 2], n * 16)
                    sp.dma_start(resid[:, bass.ds(seq(i, u, LX) * TPS, TPS), :],
                                 x[bass.ds(seq(i, u, LX), 1)].rearrange("o (a p) d -> p (o a) d", p=P)
                                 ).then_inc(x_in[u % 2], 16)
                if on(LCOPY):
                    q, b = seq(i, u, LCOPY), (u - LCOPY) % 2
                    need(sp, "h2_ok", q + 1)
                    need(sp, copied[b], turns(i, u, LCOPY, 2) * 16)
                    sp.dma_start(h2T[:, bass.ds(q * L, L)], h2[:, b, :]).then_inc(copied[b], 16)

            part_a(sp, step, LCOPY, 3 * UNROLL)
            sp.dma_start(sw1_sb[:, :], sw1[0]).then_inc(s["w_shared"], 16)
            sp.dma_start(sw2_sb[:, :], sw2[0]).then_inc(s["w_shared"], 16)
            sp.dma_start(sw3_sb[:, :, :], sw3[0].rearrange("(m p) d -> p m d", p=P)).then_inc(s["w_shared"], 16)
            sp.dma_start(rw1_sb[:, :].rearrange("p (e r) -> p e r", e=NE),
                         rw1.rearrange("e d r -> d e r")).then_inc(s["w_routed"], 16)
            sp.dma_start(rw2_sb[:, :].rearrange("p (e r) -> p e r", e=NE),
                         rw2.rearrange("e d r -> d e r")).then_inc(s["w_routed"], 16)
            sp.dma_start(rw3_sb[:, :].rearrange("p (e d) -> p e d", e=NE),
                         rw3.rearrange("e r d -> r e d")).then_inc(s["w_routed"], 16)
            sp.wait_ge(s["fill_ok"], 2)
            sp.wait_ge(s["cnt_ok"], 1)
            with sp.Fori(0, NE, 1) as e:
                n = sp.value_load(cnt_i[0:1, bass.ds(e, 1)], min_val=0, max_val=NTOK)
                sp.dma_start(lists[bass.ds(n + e * CAP, P), :].rearrange("(p a) r -> p a r", a=1),
                             fill[:, bass.ds(e, 1), :]).then_inc(s["fills_out"], 16)
            sp.wait_ge(s["fills_out"], 16 * NE)
            sp.wait_ge(s["tiles_ok"], 1)
            for r in range(UNROLL):
                sp.wait_ge(scat[r], 16 * TOPK * TPS * (NSEQ // UNROLL))

            def load_block(i):
                for quad in range(UNROLL_C):
                    g = i * UNROLL_C + quad
                    rows_of = [sp.value_load(row0_i[0:1, bass.ds(g * GT + j, 1)], min_val=0,
                                             max_val=SURPLUS + (NE - 1) * P) for j in range(GT)]
                    need(sp, "gate_ok", g - 3)
                    need(sp, "dest_ok", g - 3)
                    need(sp, "xtT_ps", g - 3)
                    for j in range(GT):
                        sp.dma_start(xt[:, quad, j:j + 1, :],
                                     lists[bass.ds(rows_of[j], P), :].rearrange("(p a) r -> p a r", a=1)
                                     ).then_inc(xt_in[quad], 16)

            load_block(0)
            with sp.Fori(1, NG // UNROLL_C, 1) as i:
                load_block(i)

            for r in range(2):
                sp.wait_ge(yout[r], 16 * GT * (NG // 2))

            def load_y(n, par):
                sp.dma_start(y0[:, par, :, :], routed[bass.ds(n * (FC * P), FC * P), :].rearrange(
                    "(a p) d -> p a d", p=P)).then_inc(y_in[par], 16)
                sp.dma_start(y1[:, par, :, :], routed[bass.ds(n * (FC * P) + NTOK, FC * P), :].rearrange(
                    "(a p) d -> p a d", p=P)).then_inc(y_in[par], 16)

            for n in range(UD):
                load_y(n, n)
            with sp.Fori(1, NTILE // FC // UD, 1) as i:
                for b in range(UD):
                    need(sp, "osum0", (i - 1) * UD + b + 1)
                    load_y(i * UD + b, b)

        @block.gpsimd
        def _(gp):
            g = nc.gpsimd
            g.memset(wout_sb[:, :, :], 0.0).then_inc(s["wout_zero"], 1)
            g.memset(ident[:, :], 0.0).then_inc(s["ident_ok"], 1)
            g.memset(pick_f[:, :, :], 0.0).then_inc(s["pick_ok"], 1)
            g.memset(head_sel[:, :], 1.0).then_inc(s["sel_ok"], 1)
            g.memset(tri[:, :], 1.0).then_inc(s["tri_ok"], 1)
            g.memset(ones_bf[:, :], 1.0).then_inc(s["consts_ok"], 1)
            g.memset(ones[:, :], 1.0).then_inc(s["consts_ok"], 1)
            g.iota(eio[:, :], [[1, NE]], base=0, channel_multiplier=0,
                   allow_small_or_imprecise_dtypes=True).then_inc(s["consts_ok"], 1)
            g.iota(expert_base[:, :], [[CAP, NE]], base=0, channel_multiplier=0,
                   allow_small_or_imprecise_dtypes=True).then_inc(s["consts_ok"], 1)
            g.iota(tok_id[:, :], [[P, NTILE]], base=NTOK, channel_multiplier=1,
                   allow_small_or_imprecise_dtypes=True).then_inc(s["consts_ok"], 1)
            g.iota(jio[:, :], [[1, RT]], base=0, channel_multiplier=0,
                   allow_small_or_imprecise_dtypes=True).then_inc(s["consts_ok"], 1)
            gp.wait_ge(s["ident_ok"], 1)
            g.affine_select(out=ident[:, :], in_=ident[:, :], compare_op=ALU.not_equal, fill=1.0, base=0,
                            pattern=[[-1, P]], channel_multiplier=1).then_inc(s["ident_ok"], 1)
            gp.wait_ge(s["pick_ok"], 1)
            g.affine_select(out=pick_f[:, :, :].rearrange("p f (h e) -> p f h e", e=E),
                            in_=pick_f[:, :, :].rearrange("p f (h e) -> p f h e", e=E),
                            compare_op=ALU.not_equal, fill=1.0, base=0,
                            pattern=[[-1, E], [-E, H], [0, E]], channel_multiplier=1).then_inc(s["pick_ok"], 1)
            gp.wait_ge(s["sel_ok"], 1)
            g.affine_select(out=head_sel[:, :], in_=head_sel[:, :], compare_op=ALU.is_ge, fill=0.0, base=0,
                            pattern=[[-E, 32]], channel_multiplier=1).then_inc(s["sel_ok"], 1)
            gp.wait_ge(s["sel_ok"], 2)
            g.affine_select(out=head_sel[:, :], in_=head_sel[:, :], compare_op=ALU.is_ge, fill=0.0, base=E - 1,
                            pattern=[[E, 32]], channel_multiplier=-1).then_inc(s["sel_ok"], 1)
            gp.wait_ge(s["tri_ok"], 1)
            g.affine_select(out=tri[:, :], in_=tri[:, :], compare_op=ALU.is_gt, fill=0.0, base=0,
                            pattern=[[1, P]], channel_multiplier=-1).then_inc(s["tri_ok"], 1)
            g.memset(fill[:, :, :], 0.0).then_inc(s["fill_zero"], 1)
            gp.wait_ge(s["fill_zero"], 1)
            g.memset(fill[:, :, C_E1:C_E1 + 1], -1.0).then_inc(s["fill_cols"], 1)
            g.iota(fill[:, :, C_ID:C_ID + 1].rearrange("p e a -> p (e a)"), [[P, NE]], base=NTOK * TOPK + NE * P,
                   channel_multiplier=1, allow_small_or_imprecise_dtypes=True).then_inc(s["fill_cols"], 1)
            gp.wait_ge(s["fill_cols"], 2)
            g.memset(pool_note[:, :], 0.0).then_inc(s["fill_ok"], 1)
            gp.wait_ge(s["surplus_out"], 16)
            g.iota(fill[:, :, C_ID:C_ID + 1].rearrange("p e a -> p (e a)"), [[P, NE]], base=NTOK * TOPK,
                   channel_multiplier=1, allow_small_or_imprecise_dtypes=True).then_inc(s["fill_ok"], 1)

            def step(i, u, on):
                if on(LC):
                    q, b = seq(i, u, LC), (u - LC) % 2
                    need(gp, "qk_ok", q + 1)
                    need(gp, "num_ps", q - 1)
                    need(gp, "den_ps", q - 1)
                    for n, f in enumerate([E] + list(range(E))):
                        need(gp, "scan_ok", q * (E + 1) + n + 1)
                        g.tensor_tensor(z[:, b, f, :], state[:, b, f, :], qk[:, b, :],
                                        ALU.mult).then_inc(s["z_ok"], 1)
                if on(LR2):
                    q, r = seq(i, u, LR2), rset(u, LR2)
                    need(gp, "rowh_ok", q + 1)
                    need(gp, "rowmeta_ok", (q + 1) * 3)
                    need_apart_pool(gp, "pos_ok", q + 1, "carrier_a", q)
                    for k in range(TOPK):
                        for j in range(TPS):
                            gp.indirect_dma_start(lists, bass.IndirectOffsetOnAxis(pos[:, r, k, j:j + 1], 0),
                                                  rows[:, r, j, :], None).then_inc(scat[r], 16)

            gp.wait_ge(s["consts_ok"], 6)
            part_a(gp, step)

            def put(i, u, on):
                if on(LY):
                    n, par = group(i, u, LY), (u - LY) % 2
                    need(gp, "y_ok", n + 1)
                    need_apart_pool(gp, "dest_ok", n + 1, "carrier_c", n)
                    for j in range(GT):
                        gp.indirect_dma_start(routed, bass.IndirectOffsetOnAxis(dest[:, (u - LY) % UNROLL_C, j:j + 1], 0),
                                              yrow[par][:, j, :], None).then_inc(yout[par], 16)

            gp.wait_ge(s["carrier_a"], NSEQ)
            part_c(gp, put)

            gp.wait_ge(s["y_ps"], NG)
            def add_ranks(n, i, b):
                need(gp, y_in[b], i * 32 + 32)
                need(gp, o_out[b], i * 16)
                g.tensor_tensor(osum[:, b, :, :], y0[:, b, :, :], y1[:, b, :, :], ALU.add).then_inc(s["osum0"], 1)

            for b in range(UD):
                add_ranks(b, 0, b)
            with gp.Fori(1, NTILE // FC // UD, 1) as i:
                for b in range(UD):
                    add_ranks(i * UD + b, i, b)

        @block.scalar
        def _(act):
            a = nc.scalar
            act.wait_ge(s["c_in"], 16)
            a.activation(c_exp[:, :], c_sb[:, :], ACT.Exp, scale=-1.0).then_inc(s["c_exp_ok"], 1)

            def centre(q, b, xn, which, name):
                for j in range(TPS):
                    a.activation(xn[:, b, j, :], resid[:, bass.ds(q * TPS + j, 1), :].rearrange("p a d -> p (a d)"),
                                 ACT.Identity, scale=rstd[:, which, j:j + 1],
                                 bias=shift[:, which, j:j + 1]).then_inc(s[name], 1)

            def step(i, u, on):
                if on(LB) or on(LE):
                    need(act, "shift_ok", seq(i, u, 0))
                if on(LB):
                    need(act, "hT_ps", seq(i, u, LB) - 1)
                if on(LE):
                    need(act, "h2T_ps", seq(i, u, LE) - 1)
                if on(LD):
                    q = seq(i, u, LD)
                    need(act, "rdT_ps", q + 1)
                    need(act, "norm_ok", q)
                    a.activation(rdenT[:, :], p_rdT, ACT.Copy).then_inc(s["rdT_ok"], 1)
                if on(LB):
                    centre(seq(i, u, LB), (u - LB) % 2, xn1, 0, "xn1_ok")
                if on(LE):
                    centre(seq(i, u, LE), (u - LE) % 2, xn2, 1, "xn2_ok")
                if on(LB):
                    q, b = seq(i, u, LB), (u - LB) % 2
                    need(act, "hT_ps", q + 1)
                    need(act, "mod_ok", 1)
                    need(act, "v_ps", q - 1)
                    a.activation(hT[:, b, :], p_hT, ACT.Identity, scale=mod[:, 1, bass.ds(q, 1)],
                                 bias=mod[:, 0, bass.ds(q, 1)]).then_inc(s["hT_ok"], 1)
                if on(LE):
                    q = seq(i, u, LE)
                    b = (u - LE) % 2
                    need(act, "h2T_ps", q + 1)
                    need(act, "log_ps", q - 1)
                    need(act, copied[b], turns(i, u, LE, 2) * 16)
                    a.activation(h2[:, b, :], p_h2T, ACT.Identity, scale=mod[:, 4, bass.ds(q, 1)],
                                 bias=mod[:, 3, bass.ds(q, 1)]).then_inc(s["h2_ok"], 1)
                if on(LD):
                    q = seq(i, u, LD)
                    need(act, "att_ps", q + 1)
                    need(act, "attb_ps", q)
                    a.activation(attT[:, :], p_att, ACT.Identity, scale=mod[:, 2, bass.ds(q, 1)],
                                 bias=ga_bout[:, bass.ds(q, 1)]).then_inc(s["attT_ok"], 1)
                if on(LB):
                    q, b = seq(i, u, LB), (u - LB) % 2
                    need(act, "qk_ps", q + 1)
                    need(act, "bq_ok", 3)
                    need(act, "feat_ok", q * 2)
                    a.activation(ex[:, 0, :], p_qk[:, 0, :], ACT.Exp, bias=q_bias[:, :]).then_inc(s["exp_ok"], 1)
                    a.activation(ex[:, 1, :], p_qk[:, 1, :], ACT.Exp, bias=bcol[:, 1:2]).then_inc(s["exp_ok"], 1)
                    need(act, "v_ps", q + 1)
                    need(act, "rep_ps", (q - 1) * 4)
                    a.activation(vT[:, b, :], p_v, ACT.Identity, bias=bcol[:, 2:3]).then_inc(s["v_ok"], 1)
                if on(LE):
                    q, r = seq(i, u, LE), rset(u, LE)
                    need(act, "log_ps", q + 1)
                    need(act, scat[r], turns(i, u, LE, UNROLL) * (16 * TOPK * TPS))
                    a.activation(rows[:, r, :, 0:D], p_back, ACT.Copy).then_inc(s["rowh_ok"], 1)
                    need(act, "sc1_ok", q - 1)
                    a.activation(rexp[:, r % 2, :, :], p_log, ACT.Exp, scale=-1.0).then_inc(s["rexp_ok"], 1)
                if on(LB):
                    q = seq(i, u, LB)
                    need(act, "feat_ok", q * 2 + 1)
                    a.activation(lnk[:, :], feat[:, 1, :], ACT.Ln).then_inc(s["lnk_ok"], 1)
                    need(act, "lnk_ok", q + 1)
                    need(act, "rk_ok", q)
                    a.activation(rk0[:, :], lnk[:, :], ACT.Exp, scale=-1.0).then_inc(s["rk0_ok"], 1)
                if on(LA) or on(LD):
                    t = seq(i, u, 0)
                    need(act, "veps1", cap(t + 1, NSEQ))
                    need(act, "veps2", t - LD + 1)
                    need(act, "rstd_ok", t)
                    a.activation(lnvar[:, :, :], var[:, :, :], ACT.Ln).then_inc(s["lnvar_ok"], 1)
                    need(act, "lnvar_ok", t + 1)
                    a.activation(rguess[:, :, :], lnvar[:, :, :], ACT.Exp, scale=-0.5).then_inc(s["rguess_ok"], 1)

            a.preload_act_table_set("natural_log_exp_and_others")
            part_a(act, step)

            for n in range(NSEQ // 4):
                act.wait_ge(s["gb_ps"], n + 1)
                a.activation(gb_rows[:, 4 * n:4 * n + 4, :], ps[:, 6 + n % 2, :].rearrange(
                    "p (k d) -> p k d", d=D), ACT.Copy).then_inc(s["gb_ok"], 1)

            def shared(i, u, on):
                if on(LH):
                    for m in range(SM):
                        n = item(i, u, LH) * SM + m
                        need(act, "sh_ps", n + 1)
                        need(act, "sh_gate", n - 1)
                        a.activation(act_s[:, m % 2, :], ps[:, m % 2, :], ACT.Silu).then_inc(s["sh_act"], 1)

            part_b(act, shared)

            def experts(i, u, on):
                if on(LT):
                    n, par = group(i, u, LT), u % 2
                    need(act, "xtT_ps", n + 1)
                    need(act, "hid_ps", n - 1)
                    a.activation(xtT[:, par, :], ps[:, 0, :], ACT.Copy).then_inc(s["xtT_ok"], 1)
                if shares(i):
                    n = (NB + i) * SM + u
                    need(act, "sh_ps", n + 1)
                    need(act, "sh_gate", n - 1)
                    a.activation(act_s[:, u % 2, :], ps[:, 4, :], ACT.Silu).then_inc(s["sh_act"], 1)
                if on(LHID):
                    n, par = group(i, u, LHID), (u - LHID) % 2
                    need(act, "hid_ps", n + 1)
                    need(act, "hidT_ps", n - 1)
                    a.activation(hid[:, par, :], ps[:, 2, :], ACT.Silu).then_inc(s["hid_act"], 1)
                if on(LG):
                    n, par = group(i, u, LG), (u - LG) % 2
                    need(act, "hidT_ps", n + 1)
                    need(act, "y_ps", n - 1)
                    a.activation(hidT[:, par, :], ps[:, 1, :], ACT.Copy).then_inc(s["hidT_ok"], 1)

            part_c(act, experts)

            def store_out(n, b):
                need(act, "osum_ok", n + 1)
                act.dma_start(out[bass.ds(n * 2, 2)].rearrange("b (a p) d -> p (b a) d", p=P),
                              osum[:, b, :, :]).then_inc(o_out[b], 16)

            with act.Fori(0, NTILE // FC // UD, 1) as i:
                for b in range(UD):
                    store_out(i * UD + b, b)
            for b in range(UD):
                act.wait_ge(o_out[b], 16 * (NTILE // FC // UD))

        @block.tensor
        def _(pe):
            mm = nc.tensor.matmul

            pe.wait_ge(s["ident_ok"], 2)
            pe.wait_ge(s["c_silu_ok"], 1)
            nc.tensor.transpose(ps[:, 0, 0:NSEQ], c_silu[:, :], ident[0:NSEQ, 0:NSEQ]).then_inc(s["cT_ps"], 1)
            pe.wait_ge(s["cT_ok"], 1)
            pe.wait_ge(s["w_mod"], 16)
            for k in range(6):
                m = mm(ps[:, 1, k * NSEQ:(k + 1) * NSEQ], wmod_sb[:, k * D:(k + 1) * D], cT[:, :],
                       start=True, stop=True)
            m.then_inc(s["mod_ps"], 1)
            pe.wait_ge(s["mod_raw"], 1)
            pe.wait_ge(s["pick_ok"], 2)
            pe.wait_ge(s["sel_ok"], 3)
            pe.wait_ge(s["tri_ok"], 2)
            pe.wait_ge(s["consts_ok"], 6)

            def pair(q, b, n):
                need(pe, "v_ok", q + 1)
                need(pe, "scan_ok", q * (E + 1) + (2 * n - 1) if n >= 2 else (q - 1) * (E + 1) + (2 * n + 7))
                for j in range(2):
                    m = mm(p_rep[:, n % 2, j * L:(j + 1) * L], pick_f[:, 2 * n + j, :], vT[:, b, :],
                           start=True, stop=True)
                m.then_inc(s["rep_ps"], 1)

            def step(i, u, on):
                if on(LC):
                    pair(seq(i, u, LC), (u - LC) % 2, 0)
                if on(LC):
                    pair(seq(i, u, LC), (u - LC) % 2, 1)
                if on(LD):
                    q = seq(i, u, LD)
                    need(pe, "rden_ok", q + 1)
                    need(pe, "rdT_ok", q)
                    for j in range(TPS):
                        for k in range(4):
                            m = mm(p_rdT[32 * k:32 * k + 32, j * P:(j + 1) * P], rden[:, j, :], ident[:, :],
                                   start=True, stop=True)
                    m.then_inc(s["rdT_ps"], 1)
                if on(LC):
                    pair(seq(i, u, LC), (u - LC) % 2, 2)
                if on(LB):
                    q, b = seq(i, u, LB), (u - LB) % 2
                    need(pe, "xn1_ok", q * TPS + TPS)
                    need(pe, "v_ok", q)
                    for j in range(TPS):
                        m = nc.tensor.transpose(p_hT[:, j * P:(j + 1) * P], xn1[:, b, j, :], ident[:, :])
                    m.then_inc(s["hT_ps"], 1)
                if on(LC):
                    pair(seq(i, u, LC), (u - LC) % 2, 3)
                if on(LE):
                    q, b = seq(i, u, LE), (u - LE) % 2
                    need(pe, "xn2_ok", q * TPS + TPS)
                    need(pe, "h2_ok", q)
                    for j in range(TPS):
                        m = nc.tensor.transpose(p_h2T[:, j * P:(j + 1) * P], xn2[:, b, j, :], ident[:, :])
                    m.then_inc(s["h2T_ps"], 1)
                if on(LD):
                    q = seq(i, u, LD)
                    need(pe, "norm_ok", q + 1)
                    need(pe, "attT_ok", q)
                    if not isinstance(q, int) or q == 0:
                        need(pe, "w_attn", 16 * (E + 2))
                    for g in range(2):
                        m = mm(p_att, wout_sb[:, g, :], num[:, g, :], start=(g == 0), stop=(g == 1))
                    m.then_inc(s["att_ps"], 1)
                if on(LB):
                    q, b = seq(i, u, LB), (u - LB) % 2
                    need(pe, "hT_ok", q + 1)
                    need(pe, "exp_ok", q * 2)
                    need(pe, "feat_ok", q * 2)
                    need(pe, "v_ok", q)
                    need(pe, "bq_ok", 3)
                    for k in range(2):
                        m = mm(p_qk[:, k, :], wqkv_sb[:, k * D:(k + 1) * D], hT[:, b, :], start=True, stop=True)
                    m.then_inc(s["qk_ps"], 1)
                if on(LD):
                    q = seq(i, u, LD)
                    need(pe, "attT_ok", q + 1)
                    need(pe, "h2_ok", q)
                    for j in range(TPS):
                        m = nc.tensor.transpose(p_attb[:, j, :], attT[:, j * P:(j + 1) * P], ident[:, :])
                    m.then_inc(s["attb_ps"], 1)
                if on(LB):
                    mm(p_v, wqkv_sb[:, 2 * D:3 * D], hT[:, (u - LB) % 2, :], start=True, stop=True).then_inc(s["v_ps"], 1)
                if on(LE):
                    q, b = seq(i, u, LE), (u - LE) % 2
                    need(pe, "h2_ok", q + 1)
                    need(pe, "rexp_ok", q)
                    need(pe, "deneps_ok", cap(q + 2, NSEQ))
                    need(pe, "carry_ok", q - 1)
                    for j in range(TPS):
                        m = nc.tensor.transpose(p_back[:, j, :], h2[:, b, j * P:(j + 1) * P], ident[:, :])
                    for j in range(TPS):
                        m = mm(p_log[:, j, :], h2[:, b, j * P:(j + 1) * P], router_sb[:, :],
                               start=True, stop=True)
                    m.then_inc(s["log_ps"], 1)
                if on(LR1):
                    n = seq(i, u, LR1) + 1
                    need(pe, "chosen_ok", n)
                    need(pe, "carry_ok", n - 1)
                    if on(LE):
                        need(pe, "rexp_ok", seq(i, u, LE) + 1)
                    for j in range(TPS):
                        mm(p_place[:, j, :], tri[:, :], chosen[:, j, :], start=True, stop=(j == 0))
                        for k in range(j):
                            mm(p_place[:, j, :], ones_bf[:, :], chosen[:, k, :], start=False, stop=(k == j - 1))
                    for j in range(TPS):
                        m = mm(p_total, ones_bf[:, :], chosen[:, j, :], start=(j == 0), stop=(j == TPS - 1))
                    m.then_inc(s["place_ps"], 1)
                if on(LC):
                    q, b = seq(i, u, LC), (u - LC) % 2
                    need(pe, "z_ok", q * (E + 1) + 1)
                    need(pe, "deneps_ok", q)
                    if on(LE):
                        need(pe, "rexp_ok", seq(i, u, LE) + 1)
                    for j in range(TPS):
                        m = mm(p_den[:, j, :], z[:, b, E, j * P:(j + 1) * P], head_sel[:, 0:H],
                               start=True, stop=True)
                    m.then_inc(s["den_ps"], 1)
                    need(pe, "norm_ok", q)
                    for g in range(2):
                        need(pe, "z_ok", q * (E + 1) + 5 + 4 * g)
                        for k in range(4):
                            m = mm(p_num[32 * k:32 * k + 32, g, :], head_sel[:, :], z[:, b, 4 * g + k, :],
                                   start=True, stop=True)
                    m.then_inc(s["num_ps"], 1)

            part_a(pe, step)

            pe.wait_ge(s["w_shared"], 48)
            for b in range(2):
                pe.wait_ge(copied[b], 16 * (NSEQ // 2))
            pe.wait_ge(s["scan_ok"], NSEQ * (E + 1))
            pe.wait_ge(s["norm_ok"], NSEQ)
            pe.wait_ge(s["feat_ok"], 2 * NSEQ)
            pe.wait_ge(s["v_ok"], NSEQ)

            pe.wait_ge(s["gb_ready"], 1)
            pe.wait_ge(s["h2_ok"], NSEQ)
            pe.wait_ge(s["x1_ok"], NSEQ)
            pe.wait_ge(s["rexp_ok"], NSEQ)
            pe.wait_ge(s["carry_ok"], NSEQ)
            for n in range(NSEQ // 4):
                need(pe, "gb_ok", n - 1)
                for k in range(4):
                    m = mm(ps[:, 6 + n % 2, k * D:(k + 1) * D],
                           mod[:, 5, 4 * n + k:4 * n + k + 1].broadcast_to([D, P]), ident[:, :],
                           start=True, stop=True)
                m.then_inc(s["gb_ps"], 1)

            def shared(i, u, on):
                if on(LH):
                    c0 = item(i, u, LH)
                    for m_ in range(SM):
                        n = c0 * SM + m_
                        need(pe, "sh_act", n - 1)
                        need(pe, "sh_gate", n - 1)
                        for w, bank in ((sw1_sb, 0), (sw2_sb, 2)):
                            m = mm(ps[:, bank + m_ % 2, :], w[:, m_ * P:(m_ + 1) * P],
                                   h2T[:, bass.ds(c0 * (FC * P), FC * P)], start=True, stop=True)
                        m.then_inc(s["sh_ps"], 1)
                if on(LO):
                    n, par = item(i, u, LO), (u - LO) % 2
                    need(pe, "sh_gate", n * SM + SM)
                    need(pe, "sh_mul", n - 1)
                    for j in range(FC):
                        for m_ in range(SM):
                            m = mm(ps[:, 4 + par, j * D:(j + 1) * D], gate_s[:, par, m_, j * P:(j + 1) * P],
                                   sw3_sb[:, m_, :], start=(m_ == 0), stop=(m_ == SM - 1))
                    m.then_inc(s["sh_out_ps"], 1)

            part_b(pe, shared)

            pe.wait_ge(s["w_routed"], 48)
            pe.wait_ge(s["tiles_ok"], 1)
            pe.wait_ge(s["sh_act"], NB * SM)
            pe.wait_ge(s["gb_ok"], NSEQ // 4)
            pe.wait_ge(s["sh_gate"], NB * SM)
            pe.wait_ge(s["sh_mul"], NB)

            def expert_columns(n):
                packed = pe.value_load(group_experts[0:1, bass.ds(n, 1)], min_val=0, max_val=NE ** GT - 1)
                return [packed // NE ** j % NE * RH for j in range(GT)]

            def experts(i, u, on):
                if on(LT):
                    n = group(i, u, LT)
                    need(pe, xt_in[u], (i + 1) * (16 * GT))
                    need(pe, "xtT_ok", n)
                    for j in range(GT):
                        m = nc.tensor.transpose(ps[:, 0, j * P:(j + 1) * P], xt[:, u, j, 0:D], ident[:, :])
                    m.then_inc(s["xtT_ps"], 1)
                if shares(i):
                    n = (NB + i) * SM + u
                    need(pe, "sh_act", n)
                    need(pe, "sh_gate", n)
                    for w, bank in ((sw1_sb, 4), (sw2_sb, 5)):
                        m = mm(ps[:, bank, :], w[:, u * P:(u + 1) * P],
                               h2T[:, bass.ds((NB + i) * (FC * P), FC * P)], start=True, stop=True)
                    m.then_inc(s["sh_ps"], 1)
                if on(LHID):
                    n, par = group(i, u, LHID), (u - LHID) % 2
                    cols = expert_columns(n)
                    need(pe, "xtT_ok", n + 1)
                    need(pe, "hid_act", n)
                    need(pe, "hid_ok", n)
                    for j in range(GT):
                        for w, bank in ((rw1_sb, 2), (rw2_sb, 3)):
                            m = mm(ps[:, bank, j * P:(j + 1) * P], xtT[:, par, j * P:(j + 1) * P],
                                   w[:, bass.ds(cols[j], RH)], start=True, stop=True)
                    m.then_inc(s["hid_ps"], 1)
                if puts_out(i, u):
                    n = NB + i - 1
                    need(pe, "sh_gate", (n + 1) * SM)
                    need(pe, "sh_mul", n)
                    for j in range(FC):
                        for m_ in range(SM):
                            m = mm(ps[:, 7, j * D:(j + 1) * D], gate_s[:, 0, m_, j * P:(j + 1) * P],
                                   sw3_sb[:, m_, :], start=(m_ == 0), stop=(m_ == SM - 1))
                    m.then_inc(s["sh_out_ps"], 1)
                if on(LY):
                    cols = expert_columns(group(i, u, LY))
                if on(LG):
                    n, par = group(i, u, LG), (u - LG) % 2
                    need(pe, "hid_ok", n + 1)
                    need(pe, "hidT_ok", n)
                    for j in range(GT):
                        m = nc.tensor.transpose(ps[:, 1, j * P:(j + 1) * P], hid[:, par, j * P:(j + 1) * P],
                                                ident[:, :])
                    m.then_inc(s["hidT_ps"], 1)
                if on(LY):
                    n, par = group(i, u, LY), (u - LY) % 2
                    need(pe, "hidT_ok", n + 1)
                    need(pe, "y_ok", n)
                    for j in range(GT):
                        m = mm(ps[:, 6, j * D:(j + 1) * D], hidT[:, par, j * P:(j + 1) * P],
                               rw3_sb[:, bass.ds(cols[j], D)], start=True, stop=True)
                    m.then_inc(s["y_ps"], 1)

            part_c(pe, experts)

        @block.vector
        def _(ve):
            v = nc.vector
            tt, ts, stt = v.tensor_tensor, v.tensor_scalar, v.scalar_tensor_tensor
            ve.wait_ge(s["c_exp_ok"], 1)
            ts(c_exp[:, :], c_exp[:, :], 1.0, None, ALU.add).then_inc(s["c_chain"], 1)
            ve.wait_ge(s["c_chain"], 1)
            v.reciprocal(c_exp[:, :], c_exp[:, :]).then_inc(s["c_chain"], 1)
            ve.wait_ge(s["c_chain"], 2)
            tt(c_silu[:, :], c_sb[:, :], c_exp[:, :], ALU.mult).then_inc(s["c_silu_ok"], 1)
            v.memset(ratio[:, :, 0:1], 0.0).then_inc(s["vconst_ok"], 1)
            v.memset(var[:, :, :], 1.0).then_inc(s["vconst_ok"], 1)
            v.memset(mv[:, :, :, :], 0.0).then_inc(s["vconst_ok"], 1)
            v.memset(rden[:, :, :], 0.0).then_inc(s["vconst_ok"], 1)
            ve.wait_ge(s["bias_in"], 16 * 5)
            ve.wait_ge(s["w_attn"], 16 * (E + 2))
            ts(wqkv_sb[:, 0:D], wqkv_sb[:, 0:D], QSCALE, None, ALU.mult).then_inc(s["bq_ok"], 1)
            ts(q_bias[:, :], bcol[:, 0:1], QSCALE, None, ALU.mult).then_inc(s["bq_ok"], 1)
            ts(k_bias1[:, :], bcol[:, 1:2], 1.0 + EPS_FEAT, None, ALU.add).then_inc(s["bq_ok"], 1)
            ve.wait_ge(s["bq_ok"], 3)
            ts(q_bias1[:, :], q_bias[:, :], 1.0 + EPS_FEAT, None, ALU.add).then_inc(s["vconst_ok"], 1)
            ve.wait_ge(s["cT_ps"], 1)
            v.tensor_copy(cT[:, :], ps[:, 0, 0:NSEQ]).then_inc(s["cT_ok"], 1)
            ve.wait_ge(s["mod_ps"], 1)
            v.tensor_copy(mod[:, :, :], ps[:, 1, 0:6 * NSEQ].rearrange("p (k b) -> p k b", k=6)
                          ).then_inc(s["mod_raw"], 1)
            ve.wait_ge(s["mod_raw"], 1)
            done = 0
            for k in (1, 4):
                ts(mod[:, k, :], mod[:, k, :], 1.0, None, ALU.add).then_inc(s["mod_chain"], 1)
                done += 1

            def gate_of(dst, src, mag, sign, n, name):
                ts(mag, src, -1.0, None, ALU.mult).then_inc(s[name], 1)
                ts(sign, src, 0.0, 2.0, ALU.is_ge, ALU.mult).then_inc(s[name], 1)
                ve.wait_ge(s[name], n + 2)
                tt(mag, mag, src, ALU.max).then_inc(s[name], 1)
                ts(sign, sign, -1.0, None, ALU.add).then_inc(s[name], 1)
                ve.wait_ge(s[name], n + 4)
                ts(mag, mag, 0.25, None, ALU.max).then_inc(s[name], 1)
                ve.wait_ge(s[name], n + 5)
                return tt(dst, mag, sign, ALU.mult)

            gate_of(mod[:, 2, :], mod[:, 2, :], mod_abs[:, :], mod_sign[:, :], done, "mod_chain"
                    ).then_inc(s["mod_chain"], 1)
            ve.wait_ge(s["mod_chain"], done + 6)
            ts(ga_bout[:, :], mod[:, 2, :], bcol[:, 3:4], None, ALU.mult).then_inc(s["mod_ok"], 1)
            gate_of(mod[:, 5, :], mod[:, 5, :], mod_abs2[:, :], mod_sign2[:, :], 0, "gb_chain").then_inc(s["gb_ready"], 1)
            ve.wait_ge(s["consts_ok"], 6)
            v.tensor_copy(carry[:, :], expert_base[:, :]).then_inc(s["carry0_ok"], 1)
            ve.wait_ge(s["carry0_ok"], 1)
            ve.wait_ge(s["vconst_ok"], 5)

            def scan(q, b, f, data):
                v.tensor_tensor_scan(state[:, b, f, :], ratio[:, b, :], data, 0.0,
                                     ALU.mult, ALU.add).then_inc(s["scan_ok"], 1)

            def pair(q, b, n):
                need(ve, "rep_ps", q * 4 + n + 1)
                for j in range(2):
                    scan(q, b, 2 * n + j, p_rep[:, n % 2, j * L:(j + 1) * L])

            def step(i, u, on):
                t = seq(i, u, 0)
                norm = on(LB) or on(LE)
                if on(LC):
                    q = seq(i, u, LC)
                    need(ve, "rk0_ok", q + 1)
                    tt(rkt[:, :], feat[:, 1, :], rk0[:, :], ALU.mult).then_inc(s["rkt_ok"], 1)
                if on(LD):
                    q = seq(i, u, LD)
                    need(ve, "den_ps", q + 1)
                    ts(den[:, :, :], p_den, EPS_DEN, None, ALU.add).then_inc(s["deneps_ok"], 1)
                if on(LC):
                    q, b = seq(i, u, LC), (u - LC) % 2
                    need(ve, "rkt_ok", q + 1)
                    stt(out=rk[:, :], in0=rkt[:, :], scalar=2.0, in1=rk0[:, :], op0=ALU.subtract,
                        op1=ALU.mult).then_inc(s["rk_ok"], 1)
                if norm:
                    need(ve, "rguess_ok", t)
                    tt(rstep1[:, :, :], rguess[:, :, :], rguess[:, :, :], ALU.mult).then_inc(s["rstep1_ok"], 1)
                if on(LD):
                    q = seq(i, u, LD)
                    need(ve, "deneps_ok", q + 1)
                    need(ve, "rdT_ps", q)
                    v.reciprocal(rden[:, :, 0:H], den[:, :, :]).then_inc(s["rden_ok"], 1)
                if norm:
                    need(ve, "rstep1_ok", t)
                    stt(out=rstep2[:, :, :], in0=rstep1[:, :, :], scalar=-0.5, in1=var[:, :, :], op0=ALU.mult,
                        op1=ALU.mult).then_inc(s["rstep2_ok"], 1)
                if on(LC):
                    need(ve, "rk_ok", q_c(i, u) + 1)
                    stt(out=ratio[:, (u - LC) % 2, 1:L], in0=feat[:, 1, 0:L - 1], scalar=-1.0, in1=rk[:, 1:L],
                        op0=ALU.mult, op1=ALU.mult).then_inc(s["ratio_ok"], 1)
                if norm:
                    need(ve, "xn1_ok", cap((t - LB) * TPS, NSEQ * TPS))
                    need(ve, "xn2_ok", (t - LE) * TPS)
                    need(ve, "rstep2_ok", t)
                    stt(out=rstd[:, :, :], in0=rstep2[:, :, :], scalar=1.5, in1=rguess[:, :, :], op0=ALU.add,
                        op1=ALU.mult).then_inc(s["rstd_ok"], 1)
                if on(LR2):
                    n = seq(i, u, LR2) + 1
                    need(ve, "place_ps", n)
                    need(ve, "carry_ok", n - 1)
                    tt(place[:, :, :], p_place, spread(carry[:, :], 1, TPS), ALU.add).then_inc(s["place_ok"], 1)
                if on(LC):
                    q, b = seq(i, u, LC), (u - LC) % 2
                    need(ve, "ratio_ok", q + 1)
                    need(ve, "z_ok", (q - 1) * (E + 1))
                    scan(q, b, E, ones[:, :])
                if norm:
                    need(ve, "rstd_ok", t)
                    stt(out=shift[:, :, :], in0=mv[:, :, :, 0:1].rearrange("p k a b -> p k (a b)"), scalar=-1.0,
                        in1=rstd[:, :, :], op0=ALU.mult, op1=ALU.mult).then_inc(s["shift_ok"], 1)
                if on(LR2):
                    need(ve, "place_ok", n)
                    tt(carry[:, :], carry[:, :], p_total, ALU.add).then_inc(s["carry_ok"], 1)
                    tt(ptmp[:, :, :, :], onehot[:, :, :, :], spread(place[:, :, :], 1, TOPK),
                       ALU.mult).then_inc(s["ptmp_ok"], 1)
                if on(LC):
                    pair(q, b, 0)
                if on(LR2):
                    need(ve, "ptmp_ok", n)
                    with nc.allow_low_precision(reason="whole numbers below 2^24, one term not zero"):
                        v.tensor_reduce(pos[:, rset(u, LR2), :, :], ptmp[:, :, :, :], AX_X,
                                        ALU.add).then_inc(s["pos_ok"], 1)
                if on(LR1):
                    m, r = seq(i, u, LR1) + 1, rset(u, LR1)
                    need(ve, "rexp_ok", m)
                    ts(score1[:, :, :], rexp[:, r % 2, :, :], 1.0, None, ALU.add).then_inc(s["sc1_ok"], 1)
                if on(LC):
                    pair(q, b, 1)
                if on(LR1):
                    need(ve, "sc1_ok", m)
                    v.reciprocal(score[:, :, :], score1[:, :, :]).then_inc(s["sc_ok"], 1)
                if on(LD):
                    need(ve, "num_ps", seq(i, u, LD) + 1)
                    need(ve, "rdT_ok", seq(i, u, LD) + 1)
                    need(ve, "att_ps", seq(i, u, LD))
                    tt(num[:, :, :], p_num, spread(rdenT[:, :], 1, 2), ALU.mult).then_inc(s["norm_ok"], 1)
                if on(LR1):
                    need(ve, "sc_ok", m)
                    tt(sel[:, :, :], score[:, :, :], spread(bias_rows[:, :], 1, TPS), ALU.add).then_inc(s["selb_ok"], 1)
                if on(LC):
                    pair(q, b, 2)
                if on(LR1):
                    need_apart(ve, "selb_ok", m)
                    for j in range(TPS):
                        v.max(top[:, j, :], sel[:, j, :]).then_inc(s["top_ok"], 1)
                if on(LC):
                    pair(q, b, 3)
                if on(LR1):
                    need_apart(ve, "top_ok", m * TPS)
                    for j in range(TPS):
                        v.max_index(topi[:, j, :], top[:, j, :], sel[:, j, :]).then_inc(s["topi_ok"], 1)
                if on(LA):
                    need_apart(ve, x_in[u % 2], turns(i, u, LA, 2) * 16 + 16)
                    bn_rows(t, 0, "stats1")
                if on(LR1):
                    need(ve, "topi_ok", m * TPS)
                    v.tensor_copy(topf[:, :, :].rearrange("p k j -> p j k"), topi[:, :, 0:TOPK]).then_inc(s["topf_ok"], 1)
                if on(LA):
                    aggregate(t, t, 0, "stats1", "aggr1")
                if on(LR1):
                    need(ve, "topf_ok", m)
                    need(ve, "ptmp_ok", m - 1)
                    tt(onehot[:, :, :, :], eio[:, :].unsqueeze(1).unsqueeze(1).broadcast_to([P, TOPK, TPS, NE]),
                       topf[:, :, :].unsqueeze(3).broadcast_to([P, TOPK, TPS, NE]),
                       ALU.is_equal).then_inc(s["onehot_ok"], 1)
                if on(LA):
                    add_eps(t, 0, "aggr1", "veps1")
                if on(LR1):
                    need(ve, "onehot_ok", m)
                    tt(chosen[:, :, :], onehot[:, 0, :, :], onehot[:, 1, :, :], ALU.add).then_inc(s["chosen_ok"], 1)
                if on(LR1):
                    tt(gtmp[:, :, :, :], onehot[:, :, :, :], spread(score[:, :, :], 1, TOPK),
                       ALU.mult).then_inc(s["gtmp_ok"], 1)
                if on(LR1):
                    v.tensor_copy(rows[:, r, :, C_E1:C_E1 + 1], topf[:, 0, :].unsqueeze(2)).then_inc(s["rowmeta_ok"], 1)
                if on(LR1):
                    v.tensor_copy(rows[:, r, :, C_ID:C_ID + 1],
                                  tok_id[:, bass.ds((m - 1) * TPS, TPS)].unsqueeze(2)).then_inc(s["rowmeta_ok"], 1)
                if on(LD):
                    qd = seq(i, u, LD)
                    need(ve, "attb_ps", qd + 1)
                    tt(resid[:, bass.ds(qd * TPS, TPS), :], resid[:, bass.ds(qd * TPS, TPS), :], p_attb,
                       ALU.add).then_inc(s["x1_ok"], 1)
                if on(LB):
                    ql = seq(i, u, LB)
                    need(ve, "exp_ok", ql * 2 + 2)
                    ts(ex[:, :, :], ex[:, :, :], 1.0, EPS_FEAT, ALU.min, ALU.add).then_inc(s["exmin_ok"], 1)
                if on(LR1):
                    need(ve, "gtmp_ok", m)
                    v.tensor_reduce(rows[:, r, :, C_G1:C_G2 + 1].rearrange("p j k -> p k j"), gtmp[:, :, :, :],
                                    AX_X, ALU.add).then_inc(s["rowmeta_ok"], 1)
                if on(LD):
                    need_apart(ve, "x1_ok", qd + 1)
                    bn_rows(qd, 1, "stats2")
                if on(LB):
                    need(ve, "exmin_ok", ql + 1)
                    for k, bias in ((1, k_bias1), (0, q_bias1)):
                        stt(out=feat[:, k, :], in0=p_qk[:, k, :], scalar=bias[:, :], in1=ex[:, k, :],
                            op0=ALU.add, op1=ALU.max).then_inc(s["feat_ok"], 1)
                if on(LD):
                    aggregate(t, qd, 1, "stats2", "aggr2")
                if on(LB):
                    need(ve, "feat_ok", ql * 2 + 2)
                    need(ve, "z_ok", (ql - 1) * (E + 1))
                    tt(qk[:, (u - LB) % 2, :], feat[:, 0, :], feat[:, 1, :], ALU.mult).then_inc(s["qk_ok"], 1)
                if on(LD):
                    add_eps(qd, 1, "aggr2", "veps2")

            def q_c(i, u):
                return seq(i, u, LC)

            def bn_rows(q, which, done):
                for j in range(TPS):
                    v.bn_stats(stats[:, which, j, :],
                               resid[:, bass.ds(q * TPS + j, 1), :].rearrange("p a d -> p (a d)")).then_inc(s[done], 1)

            def aggregate(t, q, which, stats_done, done):
                need(ve, "shift_ok", t)
                need_apart(ve, stats_done, q * TPS + TPS)
                for j in range(TPS):
                    v.bn_aggr(mv[:, which, j, :], stats[:, which, j, :]).then_inc(s[done], 1)

            def add_eps(q, which, aggr_done, done):
                need(ve, aggr_done, q * TPS + TPS)
                ts(var[:, which, :], mv[:, which, :, 1:2].rearrange("p a b -> p (a b)"), EPS_LN, None,
                   ALU.add).then_inc(s[done], 1)

            part_a(ve, step)

            links = [0]

            def link(ins):
                links[0] += 1
                ins.then_inc(s["tb"], 1)
                ve.wait_ge(s["tb"], links[0])

            ve.wait_ge(s["carry_ok"], NSEQ)
            link(tt(cnt[:, :], carry[:, :], expert_base[:, :], ALU.subtract))
            v.tensor_copy(cnt_i[:, :], cnt[:, :]).then_inc(s["cnt_ok"], 1)
            link(ts(nt_f[:, :], cnt[:, :], 1.0 / P, (P - 1.0) / P - (P - 1.0) / (2 * P), ALU.mult, ALU.add))
            link(v.tensor_copy(nt_i[:, :], nt_f[:, :]))
            link(v.tensor_copy(nt[:, :], nt_i[:, :]))
            link(v.tensor_tensor_scan(end[:, :], ones[:, 0:NE], nt[:, :], 0.0, ALU.mult, ALU.add))
            link(tt(offt[:, 0:NE], end[:, :], nt[:, :], ALU.subtract))
            link(stt(out=off[:, 0:NE], in0=offt[:, 0:NE], scalar=-float(P), in1=expert_base[:, :],
                     op0=ALU.mult, op1=ALU.add))
            link(ts(off[:, NE:NE + 1], end[:, NE - 1:NE], -float(P), float(SURPLUS), ALU.mult, ALU.add))
            link(tt(doff[:, :], off[:, 1:NE + 1], off[:, 0:NE], ALU.subtract))
            link(tt(past[:, :, :], jio[:, :].unsqueeze(2).broadcast_to([P, RT, NE]), spread(end[:, :], 1, RT),
                    ALU.is_ge))
            link(v.tensor_reduce(et[:, :], past[:, :, :], AX_X, ALU.add))
            link(ts(etw[:, :], et[:, :], NE - 1.0, None, ALU.min))
            for j in range(1, GT):
                link(ts(etw[:, :].rearrange("p (n j) -> p j n", j=GT)[:, j, :],
                        etw[:, :].rearrange("p (n j) -> p j n", j=GT)[:, j, :], float(NE ** j), None, ALU.mult))
            link(v.tensor_reduce(packed_f[:, :], etw[:, :].rearrange("p (n j) -> p n j", j=GT), AX_X, ALU.add))
            link(v.tensor_copy(group_experts[:, :], packed_f[:, :]))
            link(tt(past[:, :, :], past[:, :, :], spread(doff[:, :], 1, RT), ALU.mult))
            link(v.tensor_reduce(row0[:, :], past[:, :, :], AX_X, ALU.add))
            link(stt(out=row0b[:, :], in0=jio[:, :], scalar=float(P), in1=row0[:, :], op0=ALU.mult, op1=ALU.add))
            link(ts(row0[:, :], row0b[:, :], off[:, 0:1], None, ALU.add))
            v.tensor_copy(row0_i[:, :], row0[:, :]).then_inc(s["tiles_ok"], 1)
            ve.wait_ge(s["gb_ok"], NSEQ // 4)

            def add_shared(n, bank):
                need(ve, "sh_out_ps", n + 1)
                need(ve, "sh_mul", n)
                for k in range(2):
                    gb = gb_rows[:, bass.ds(n * 2 + k, 1), :].broadcast_to([P, TPS, D])
                    tt(sh_mul[:, k * TPS:(k + 1) * TPS, :],
                       bank[:, k * L:(k + 1) * L].rearrange("p (a d) -> p a d", d=D), gb,
                       ALU.mult).then_inc(s["sh_half"], 1)
                need(ve, "sh_half", n * 2 + 2)
                tt(resid[:, bass.ds(n * FC, FC), :], resid[:, bass.ds(n * FC, FC), :], sh_mul[:, :, :],
                   ALU.add).then_inc(s["sh_mul"], 1)

            def shared(i, u, on):
                if on(LH):
                    par = u % 2
                    need(ve, "sh_out_ps", item(i, u, LH) - 1)
                    for m in range(SM):
                        n = item(i, u, LH) * SM + m
                        need(ve, "sh_act", n + 1)
                        need(ve, "sh_ps", n + 1)
                        tt(gate_s[:, par, m, :], act_s[:, m % 2, :], ps[:, 2 + m % 2, :],
                           ALU.mult).then_inc(s["sh_gate"], 1)
                if on(LO):
                    add_shared(item(i, u, LO), ps[:, 4 + (u - LO) % 2, :])

            part_b(ve, shared)

            def experts(i, u, on):
                if shares(i):
                    if u == 0:
                        need(ve, "sh_out_ps", NB + i)
                    m = (NB + i) * SM + u
                    need(ve, "sh_act", m + 1)
                    need(ve, "sh_ps", m + 1)
                    tt(gate_s[:, 0, u, :], act_s[:, u % 2, :], ps[:, 5, :], ALU.mult).then_inc(s["sh_gate"], 1)
                if on(LHID):
                    n, par = group(i, u, LHID), (u - LHID) % 2
                    need(ve, "hid_act", n + 1)
                    need(ve, "hid_ps", n + 1)
                    tt(hid[:, par, :], hid[:, par, :], ps[:, 3, :], ALU.mult).then_inc(s["hid_ok"], 1)
                if on(LHID):
                    quad = (u - LHID) % UNROLL_C
                    e1, id2, g1, g2 = (xt[:, quad, :, k:k + 1].rearrange("p j a -> p (j a)")
                                       for k in (C_E1, C_ID, C_G1, C_G2))
                    block_of, half = i + (u - LHID) // UNROLL_C, i * (UNROLL_C // 2) + (u - LHID) // 2
                    need(ve, xt_in[quad], (block_of + 1) * (16 * GT))
                    need(ve, "gate_ok", n)
                    need(ve, "dest_ok", n)
                    tt(first[:, :], e1, et[:, bass.ds(n * GT, GT)], ALU.is_equal).then_inc(s["first_ok"], 1)
                    tt(gdiff[:, :], g1, g2, ALU.subtract).then_inc(s["gdiff_ok"], 1)
                if on(LY):
                    ny, par = group(i, u, LY), (u - LY) % 2
                    need(ve, "y_ps", ny + 1)
                    need(ve, yout[par], (i * (UNROLL_C // 2) + (u - LY) // 2) * (16 * GT))
                    tt(yrow[par][:, :, :], ps[:, 6, :].rearrange("p (j d) -> p j d", d=D),
                       gate[:, (u - LY) % UNROLL_C, :].unsqueeze(2).broadcast_to([P, GT, D]),
                       ALU.mult).then_inc(s["y_ok"], 1)
                if on(LHID):
                    need(ve, "first_ok", n + 1)
                    need(ve, "gdiff_ok", n + 1)
                    tt(gsel[:, :], first[:, :], gdiff[:, :], ALU.mult).then_inc(s["gsel_ok"], 1)
                    need(ve, yout[(u - LHID) % 2], (half - 1) * (16 * GT))
                    stt(out=dest[:, quad, :], in0=first[:, :], scalar=-float(NTOK), in1=id2,
                        op0=ALU.mult, op1=ALU.add).then_inc(s["dest_ok"], 1)
                if puts_out(i, u):
                    add_shared(NB + i - 1, ps[:, 7, :])
                if on(LHID):
                    need(ve, "gsel_ok", n + 1)
                    need(ve, "y_ok", n - 3)
                    tt(gate[:, quad, :], gsel[:, :], g2, ALU.add).then_inc(s["gate_ok"], 1)

            part_c(ve, experts)

            def total(i, u, on):
                if on(0):
                    n = i * UD + u
                    need(ve, "osum0", n + 1)
                    for k in range(2):
                        gb = gb_rows[:, bass.ds(n * 2 + k, 1), :].broadcast_to([P, TPS, D])
                        part = osum[:, u, k * TPS:(k + 1) * TPS, :]
                        tt(part, part, gb, ALU.mult).then_inc(s["osum1"], 1)
                if on(1):
                    n, b = i * UD + u - 1, (u - 1) % UD
                    need(ve, "osum1", n * 2 + 2)
                    tt(osum[:, b, :, :], osum[:, b, :, :], resid[:, bass.ds(n * FC, FC), :],
                       ALU.add).then_inc(s["osum_ok"], 1)

            pipeline(ve, total, NTILE // FC, UD, 1, UD)


_INS = ["L0_attn_x", "L0_attn_W_qkv", "L0_attn_b_qkv", "L0_attn_W_out", "L0_attn_b_out", "L0_ffn_router_w",
        "L0_ffn_expert_bias", "L0_ffn_shared_w1", "L0_ffn_shared_w2", "L0_ffn_shared_w3", "L0_ffn_routed_w1",
        "L0_ffn_routed_w2", "L0_ffn_routed_w3", "L0_c", "L0_wmod"]


def kernel(**inputs):
    import numpy as np
    import concourse.bacc as bacc
    from concourse.bass_utils import run_bass_kernel_spmd

    nc = bacc.Bacc("TRN2", target_bir_lowering=False, num_devices=1)
    arrays, args = {}, []
    for name in _INS:
        a = np.ascontiguousarray(inputs[name])
        arrays[f"in_{name}"] = a
        args.append(nc.dram_tensor(f"in_{name}", a.shape, mybir.dt.from_np(a.dtype), kind="ExternalInput").ap())
    args.append(nc.dram_tensor("out_x", (NSEQ, L, D), F32, kind="ExternalOutput").ap())
    adaln_block(nc, *args)
    result = run_bass_kernel_spmd(nc, [arrays], core_ids=[0])
    return result.results[0]["out_x"]
```
